# Optimizing a Trainium2 kernel written in Bass

```python
import numpy as np
import jax
import jax.numpy as jnp

def _softmax(x, axis=-1):
    return jax.nn.softmax(x, axis=axis)

def _gelu(x):
    return jax.nn.gelu(x, approximate=True)

def _silu(x):
    return jax.nn.silu(x)

def _sigmoid(x):
    return jax.nn.sigmoid(x)

def _layernorm(x, axis=-1, eps=1e-05):
    m = jnp.mean(x, axis=axis, keepdims=True)
    v = jnp.var(x, axis=axis, keepdims=True)
    return (x - m) / jnp.sqrt(v + eps)

def _scatter_add(tgt, idx, src, axis=0):
    return tgt.at[idx].add(src)

def _segment_sum(src, seg, n):
    return jax.ops.segment_sum(src, seg, n)
kernel_name = 'mk_xattn_seq_d2_seqx_r8_27a5d9'

def setup_inputs(seed: int=0):
    np.random.seed(seed)
    _w = jnp.asarray

    def _rec_inputs():
        import jax
        import jax.numpy as jnp
        _rk = jax.random.key(seed)
        x = -0.0003929 + 0.9999 * jax.random.normal(jax.random.fold_in(_rk, 1), (32, 64, 512), jnp.float32)
        _lenS = 64 - jax.random.randint(jax.random.fold_in(_rk, 7), (32,), 0, max(1, 64 // 4) + 1, jnp.int32)
        _lenS2 = 64 - jax.random.randint(jax.random.fold_in(_rk, 8), (32,), 0, max(1, 64 // 4) + 1, jnp.int32)
        _ctx_4096P = jax.random.normal(jax.random.fold_in(_rk, 11), (32, 16, 512), jnp.float32)
        _ctx_4096c = jax.random.dirichlet(jax.random.fold_in(_rk, 511), 0.3 * jnp.ones((16,), jnp.float32), (32, 64))
        _ctx_4096t = jnp.einsum('bsk,bkd->bsd', _ctx_4096c, _ctx_4096P)
        _ctx_4096t = _ctx_4096t * jax.lax.rsqrt(jnp.mean(jnp.square(_ctx_4096t)) + 1e-12) * 0.953939
        ctx_4096 = 2.81802e-05 + 1.00001 * (_ctx_4096t + 0.3 * jax.random.normal(jax.random.fold_in(_rk, 611), (32, 64, 512), jnp.float32))
        _validS = jnp.arange(64)[None, :] < _lenS[:, None]
        _validS2 = jnp.arange(64)[None, :] < _lenS2[:, None]
        _causal = jnp.tril(jnp.ones((64, 64), dtype=bool))
        mask_Bx1x4096_ff1 = jnp.where(jnp.ones((32, 1, 512), dtype=bool), 1.0, 0.0).astype(jnp.float32)
        return (x, ctx_4096, mask_Bx1x4096_ff1)
    x, ctx_4096, mask_Bx1x4096_ff1 = _rec_inputs()

    def _L0_xattn_setup():
        import jax, jax.numpy as jnp
        import numpy as np
        H = 512
        NH = 32
        NKV = 8
        HD = H // NH
        R = 16
        SCALING = 32.0 / 16.0

        def _lora_linear(x, W, A, B):
            return x @ W + SCALING * (x @ A @ B)
        key = jax.random.key(seed)
        ks = jax.random.split(key, 16)
        d = {'hidden_states': jax.random.normal(ks[0], (4, 128, H), jnp.float32), 'traces': jax.random.normal(ks[1], (4, 128, H), jnp.float32), 'Wq': jax.random.normal(ks[2], (H, H), jnp.float32) * 0.02, 'Aq': jax.random.normal(ks[3], (H, R), jnp.float32) * 0.02, 'Bq': jax.random.normal(ks[4], (R, H), jnp.float32) * 0.02, 'Wk': jax.random.normal(ks[5], (H, NKV * HD), jnp.float32) * 0.02, 'Ak': jax.random.normal(ks[6], (H, R), jnp.float32) * 0.02, 'Bk': jax.random.normal(ks[7], (R, NKV * HD), jnp.float32) * 0.02, 'Wv': jax.random.normal(ks[8], (H, NKV * HD), jnp.float32) * 0.02, 'Av': jax.random.normal(ks[9], (H, R), jnp.float32) * 0.02, 'Bv': jax.random.normal(ks[10], (R, NKV * HD), jnp.float32) * 0.02, 'Wo': jax.random.normal(ks[11], (H, H), jnp.float32) * 0.02, 'Ao': jax.random.normal(ks[12], (H, R), jnp.float32) * 0.02, 'Bo': jax.random.normal(ks[13], (R, H), jnp.float32) * 0.02}
        return d
    _L0_xattn_all = _L0_xattn_setup()
    _L0_xattn_in = {k: v for k, v in _L0_xattn_all.items() if k in ('Wq', 'Aq', 'Bq', 'Wk', 'Ak', 'Bk', 'Wv', 'Av', 'Bv', 'Wo', 'Ao', 'Bo')}
    del _L0_xattn_all

    def _L1_xattn_setup():
        import jax, jax.numpy as jnp
        import numpy as np
        NUM_HEADS = 8
        CHUNK = 64
        EPS = 1e-05
        NEG = -1000000000.0

        def _chunk_attn(q, k, v, masks, W_in, b_in, W_out, b_out):
            N, C, T = q.shape
            H, Dh = (NUM_HEADS, C // NUM_HEADS)
            nc = T // CHUNK
            Wq, Wk, Wv = jnp.split(W_in, 3, axis=0)
            bq, bk, bv = jnp.split(b_in, 3, axis=0)

            def proj(t, W, b):
                t = t.transpose(0, 2, 1) @ W.T + b
                return t.reshape(N, nc, CHUNK, H, Dh)
            qh = proj(q, Wq, bq)
            kh = proj(k, Wk, bk)
            vh = proj(v, Wv, bv)
            scale = 1.0 / jnp.sqrt(jnp.asarray(Dh, q.dtype))
            scores = jnp.einsum('bnqhd,bnkhd->bnhqk', qh, kh) * scale
            km = masks[:, 0, :].reshape(N, nc, CHUNK)
            scores = scores + jnp.where(km[:, :, None, None, :] > 0, 0.0, NEG)
            attn = jax.nn.softmax(scores, axis=-1)
            out = jnp.einsum('bnhqk,bnkhd->bnqhd', attn, vh).reshape(N, T, C)
            out = out @ W_out.T + b_out
            out = out.transpose(0, 2, 1) * masks
            return out
        key = jax.random.key(seed)
        ks = jax.random.split(key, 8)
        N, C, T = (4, 64, 512)
        x = jax.random.normal(ks[0], (N, C, T), dtype=jnp.float32)
        q = jax.random.normal(ks[1], (N, C, T), dtype=jnp.float32)
        k = jax.random.normal(ks[2], (N, C, T), dtype=jnp.float32)
        v = jax.random.normal(ks[3], (N, C, T), dtype=jnp.float32)
        masks = jnp.ones((N, 1, T), dtype=jnp.float32)
        s = 1.0 / np.sqrt(C)
        W_in = jax.random.normal(ks[4], (3 * C, C), dtype=jnp.float32) * s
        b_in = jnp.zeros((3 * C,), dtype=jnp.float32)
        W_out = jax.random.normal(ks[5], (C, C), dtype=jnp.float32) * s
        b_out = jnp.zeros((C,), dtype=jnp.float32)
        return {'x': x, 'q': q, 'k': k, 'v': v, 'masks': masks, 'W_in': W_in, 'b_in': b_in, 'W_out': W_out, 'b_out': b_out}
    _L1_xattn_all = _L1_xattn_setup()
    _L1_xattn_in = {k: v for k, v in _L1_xattn_all.items() if k in ('W_in', 'b_in', 'W_out', 'b_out')}
    del _L1_xattn_all
    return {'x': x, 'ctx_4096': ctx_4096, 'mask_Bx1x4096_ff1': mask_Bx1x4096_ff1, 'L0_xattn_Wq': _L0_xattn_in['Wq'], 'L0_xattn_Aq': _L0_xattn_in['Aq'], 'L0_xattn_Bq': _L0_xattn_in['Bq'], 'L0_xattn_Wk': _L0_xattn_in['Wk'], 'L0_xattn_Ak': _L0_xattn_in['Ak'], 'L0_xattn_Bk': _L0_xattn_in['Bk'], 'L0_xattn_Wv': _L0_xattn_in['Wv'], 'L0_xattn_Av': _L0_xattn_in['Av'], 'L0_xattn_Bv': _L0_xattn_in['Bv'], 'L0_xattn_Wo': _L0_xattn_in['Wo'], 'L0_xattn_Ao': _L0_xattn_in['Ao'], 'L0_xattn_Bo': _L0_xattn_in['Bo'], 'L1_xattn_W_in': _L1_xattn_in['W_in'], 'L1_xattn_b_in': _L1_xattn_in['b_in'], 'L1_xattn_W_out': _L1_xattn_in['W_out'], 'L1_xattn_b_out': _L1_xattn_in['b_out']}

def reference(x, ctx_4096, mask_Bx1x4096_ff1, L0_xattn_Wq, L0_xattn_Aq, L0_xattn_Bq, L0_xattn_Wk, L0_xattn_Ak, L0_xattn_Bk, L0_xattn_Wv, L0_xattn_Av, L0_xattn_Bv, L0_xattn_Wo, L0_xattn_Ao, L0_xattn_Bo, L1_xattn_W_in, L1_xattn_b_in, L1_xattn_W_out, L1_xattn_b_out):
    import jax
    import jax.numpy as jnp

    def _L0_xattn_ref(hidden_states, traces, Wq, Aq, Bq, Wk, Ak, Bk, Wv, Av, Bv, Wo, Ao, Bo):
        import jax, jax.numpy as jnp
        import numpy as np
        H = 512
        NH = 32
        NKV = 8
        HD = H // NH
        R = 16
        SCALING = 32.0 / 16.0

        def _lora_linear(x, W, A, B):
            return x @ W + SCALING * (x @ A @ B)
        bsz, q_len, _ = hidden_states.shape
        t_len = traces.shape[1]
        groups = NH // NKV
        q = _lora_linear(hidden_states, Wq, Aq, Bq).reshape(bsz, q_len, NH, HD)
        q = jnp.transpose(q, (0, 2, 1, 3))
        k = _lora_linear(traces, Wk, Ak, Bk).reshape(bsz, t_len, NKV, HD)
        v = _lora_linear(traces, Wv, Av, Bv).reshape(bsz, t_len, NKV, HD)
        k = jnp.transpose(k, (0, 2, 1, 3))
        v = jnp.transpose(v, (0, 2, 1, 3))
        k = jnp.repeat(k, groups, axis=1)
        v = jnp.repeat(v, groups, axis=1)
        scores = jnp.einsum('bhqd,bhtd->bhqt', q, k) / jnp.sqrt(jnp.asarray(HD, q.dtype))
        attn = jax.nn.softmax(scores, axis=-1)
        context = jnp.einsum('bhqt,bhtd->bhqd', attn, v)
        context = jnp.transpose(context, (0, 2, 1, 3)).reshape(bsz, q_len, H)
        out = _lora_linear(context, Wo, Ao, Bo)
        return hidden_states + out

    def _L1_xattn_ref(x, q, k, v, masks, W_in, b_in, W_out, b_out):
        import jax, jax.numpy as jnp
        import numpy as np
        NUM_HEADS = 8
        CHUNK = 64
        EPS = 1e-05
        NEG = -1000000000.0

        def _chunk_attn(q, k, v, masks, W_in, b_in, W_out, b_out):
            N, C, T = q.shape
            H, Dh = (NUM_HEADS, C // NUM_HEADS)
            nc = T // CHUNK
            Wq, Wk, Wv = jnp.split(W_in, 3, axis=0)
            bq, bk, bv = jnp.split(b_in, 3, axis=0)

            def proj(t, W, b):
                t = t.transpose(0, 2, 1) @ W.T + b
                return t.reshape(N, nc, CHUNK, H, Dh)
            qh = proj(q, Wq, bq)
            kh = proj(k, Wk, bk)
            vh = proj(v, Wv, bv)
            scale = 1.0 / jnp.sqrt(jnp.asarray(Dh, q.dtype))
            scores = jnp.einsum('bnqhd,bnkhd->bnhqk', qh, kh) * scale
            km = masks[:, 0, :].reshape(N, nc, CHUNK)
            scores = scores + jnp.where(km[:, :, None, None, :] > 0, 0.0, NEG)
            attn = jax.nn.softmax(scores, axis=-1)
            out = jnp.einsum('bnhqk,bnkhd->bnqhd', attn, vh).reshape(N, T, C)
            out = out @ W_out.T + b_out
            out = out.transpose(0, 2, 1) * masks
            return out
        out = _chunk_attn(q, k, v, masks, W_in, b_in, W_out, b_out) + x
        mu = jnp.mean(out, axis=2, keepdims=True)
        var = jnp.mean(jnp.square(out - mu), axis=2, keepdims=True)
        return (out - mu) * jax.lax.rsqrt(var + EPS)
    x = _L0_xattn_ref(x, ctx_4096, L0_xattn_Wq, L0_xattn_Aq, L0_xattn_Bq, L0_xattn_Wk, L0_xattn_Ak, L0_xattn_Bk, L0_xattn_Wv, L0_xattn_Av, L0_xattn_Bv, L0_xattn_Wo, L0_xattn_Ao, L0_xattn_Bo)
    x = _L1_xattn_ref(x, ctx_4096, ctx_4096, ctx_4096, mask_Bx1x4096_ff1, L1_xattn_W_in, L1_xattn_b_in, L1_xattn_W_out, L1_xattn_b_out)
    return x

_drawn_inputs = setup_inputs


def setup_inputs(seed=0):
    import zlib

    import numpy as np

    out = dict(_drawn_inputs(seed))
    spreads = {'L1_xattn_b_in': (0.0, 0.48), 'L1_xattn_b_out': (0.0, 0.8)}
    factors = {'L0_xattn_Wq': 7.082,
     'L0_xattn_Aq': 8.0,
     'L0_xattn_Bq': 8.0,
     'L0_xattn_Wk': 7.044,
     'L0_xattn_Ak': 8.0,
     'L0_xattn_Bk': 8.0,
     'L0_xattn_Av': 3.486,
     'L0_xattn_Bv': 3.49,
     'L0_xattn_Ao': 3.5,
     'L0_xattn_Bo': 3.532}
    for name, (base, spread) in spreads.items():
        noise = np.random.default_rng([zlib.crc32(name.encode()), seed]).standard_normal(out[name].shape)
        drawn = base * np.exp(spread * noise) if base else spread * noise
        out[name] = jnp.asarray(drawn.astype(out[name].dtype))
    for name, factor in factors.items():
        out[name] = (out[name] * factor).astype(out[name].dtype)
    return out
```

```python
from contextlib import ExitStack

import concourse.bass as bass
from concourse import mybir

F32 = mybir.dt.float32
F32R = mybir.dt.float32r
BF16 = mybir.dt.bfloat16
ACT = mybir.ActivationFunctionType
ALU = mybir.AluOpType
AX_X = mybir.AxisListType.X

N, S, H = 32, 64, 512
PAIRS = N // 2
P = 128
KT = H // P
NKV, REP, HD = 8, 4, 16
R = 16
CH, NC, NH1, HD1 = 64, 8, 8, 8
QD = 32
SCALE0 = HD ** -0.5
SCALE1 = HD1 ** -0.5
LORA = 2.0
EPS = 1e-5
PARTS = 3
MROWS = 32 * PARTS
UNITS1, UNITS0 = NC, 4
UNITS = UNITS1 + UNITS0
RING = 4


def build(nc, xT, xn, cT, cn, mask, wq, aqT, bq, wkv, akvT, bkv, wo, aoT, bo,
          w1q, w1k, w1v, b1q, b1k, b1v, w1o, w1bias, b1o,
          sel0, selq, selk, fold0, fold1, negc, ones0, ones1, ident, out):
    with ExitStack() as ctx:
        def sb(name, shape, dt=F32):
            return ctx.enter_context(nc.sbuf_tensor(name, shape, dt))

        def ps(name, dt=F32):
            return ctx.enter_context(nc.psum_tensor(name, [P, 2048 // (4 if dt == F32 else 2)], dt))

        def sem(name):
            return ctx.enter_context(nc.semaphore(name))

        masked_dram = nc.dram_tensor("masked_rows", (PARTS, N, H), BF16, kind="Internal").ap()

        wq_sb = sb("wq_sb", [P, KT, REP, P])
        wkv_sb = sb("wkv_sb", [P, KT, 2, P])
        wo_sb = sb("wo_sb", [P, REP, H])
        aqT_sb = sb("aqT_sb", [R, KT, P])
        bq_sb = sb("bq_sb", [R, H])
        akvT_sb = sb("akvT_sb", [R, 2, KT, P])
        bkv_sb = sb("bkv_sb", [R, 2, P])
        aoT_sb = sb("aoT_sb", [R, REP, P])
        bo_sb = sb("bo_sb", [R, H])
        w1q_sb = sb("w1q_sb", [P, P])
        w1k_sb = sb("w1k_sb", [P, P])
        w1v_sb = sb("w1v_sb", [P, P])
        w1o_sb = sb("w1o_sb", [P, S])
        b1_sb = sb("b1_sb", [P, 4])
        b1v_sb = sb("b1v_sb", [S, 1])
        w1bias_sb = sb("w1bias_sb", [S, P])
        sel0_sb = sb("sel0_sb", [P, NKV])
        selq_sb = sb("selq_sb", [P, 4])
        selk_sb = sb("selk_sb", [P, 4])
        fold0_sb = sb("fold0_sb", [MROWS, 2, 2, 4, P], BF16)
        fold1_sb = sb("fold1_sb", [P, 2, NC, 2, 2, CH], BF16)
        negc_sb = sb("negc_sb", [P, P], BF16)
        ones0_sb = sb("ones0_sb", [P, QD])
        ident_sb = sb("ident_sb", [P, P], BF16)
        mask_sb = sb("mask_sb", [N, H])
        masked_sb = sb("masked_sb", [N, H], BF16)

        xT_sb = sb("xT_sb", [P, KT, P])
        cT_sb = sb("cT_sb", [P, KT, P])
        xn_sb = sb("xn_sb", [P, H])
        cn_sb = sb("cn_sb", [P, H])
        mk_sb = sb("mk_sb", [P, H])

        q0h = sb("q0h", [P, 2, REP, S], F32R)
        q0l = sb("q0l", [P, 2, REP, S], F32R)
        k0h = sb("k0h", [P, 2, S], F32R)
        k0l = sb("k0l", [P, 2, S], F32R)
        kb0h = sb("kb0h", [P, 2, NKV, S], F32R)
        kb0l = sb("kb0l", [P, 2, NKV, S], F32R)
        v0b = sb("v0b", [P, 2, 4, QD])
        m0 = sb("m0", [P, 32])
        m0p = sb("m0p", [P, PARTS, 32], BF16)
        m0r = sb("m0r", [P, 2, 32])
        mT0 = sb("mT0", [MROWS, P], BF16)
        rec0 = sb("rec0", [P, H])
        o0 = sb("o0", [P, REP, 2, S])

        q1h = sb("q1h", [P, H], F32R)
        q1l = sb("q1l", [P, H], F32R)
        k1h = sb("k1h", [P, H], F32R)
        k1l = sb("k1l", [P, H], F32R)
        qm1h = sb("qm1h", [P, NC, 4, CH], F32R)
        qm1l = sb("qm1l", [P, NC, 4, CH], F32R)
        kb1h = sb("kb1h", [P, NC, 4, CH], F32R)
        kb1l = sb("kb1l", [P, NC, 4, CH], F32R)
        v1b = sb("v1b", [P, NC, 2, 4, QD])
        m1 = sb("m1", [P, 2, 32])
        m1p = sb("m1p", [P, 2, PARTS, 32], BF16)
        m1r = sb("m1r", [P, 2, 2, 32])
        mT1 = sb("mT1", [P, 2, P], BF16)
        sum1 = sb("sum1", [P, H])
        rec1 = sb("rec1", [P, H])
        o1n = sb("o1n", [P, 2, 2, 4 * CH])

        pT = sb("pT", [P, RING, H])

        y1 = sb("y1", [P, H])
        z = sb("z", [P, H])
        stats = sb("stats", [P, 6])
        mv = sb("mv", [P, 2])
        vare = sb("vare", [P, 1])
        minus_half = sb("minus_half", [P, 1])
        rstd = sb("rstd", [P, 1])
        res = sb("res", [P, H])

        SN = [ps("sn0"), ps("sn1")]
        ST = [ps("st0"), ps("st1")]
        PR = [ps("pr0"), ps("pr1")]
        PV = [ps("pv0"), ps("pv1")]

        ld_w = sem("ld_w")
        ld_x = sem("ld_x")
        ld_c = sem("ld_c")
        ld_cn = sem("ld_cn")
        ld_xn = sem("ld_xn")
        ld_mk = sem("ld_mk")
        ld_km = sem("ld_km")
        st_km = sem("st_km")
        st_out = sem("st_out")
        set_dve = sem("set_dve")
        set_act = sem("set_act")
        set_pool = sem("set_pool")
        set_pe = sem("set_pe")
        pe_kv0 = sem("pe_kv0")
        pe_q0 = sem("pe_q0")
        pe_sn = sem("pe_sn")
        pe_qk1 = sem("pe_qk1")
        pe_v1 = sem("pe_v1")
        pe_mt = sem("pe_mt")
        pe_st = sem("pe_st")
        pe_pv = sem("pe_pv")
        pe_o1 = sem("pe_o1")
        pe_o0 = sem("pe_o0")
        ac_q0h = sem("ac_q0h")
        ac_k0h = sem("ac_k0h")
        ac_v0 = sem("ac_v0")
        ac_qk1h = sem("ac_qk1h")
        ac_mt = sem("ac_mt")
        ac_ex = sem("ac_ex")
        ac_v1 = sem("ac_v1")
        ac_m1 = sem("ac_m1")
        dv_q0l = sem("dv_q0l")
        dv_k0l = sem("dv_k0l")
        dv_kb0h = sem("dv_kb0h")
        dv_mx = sem("dv_mx")
        dv_p1 = sem("dv_p1")
        dv_p0 = sem("dv_p0")
        dv_qk1l = sem("dv_qk1l")
        dv_s1 = sem("dv_s1")
        dv_r1 = sem("dv_r1")
        dv_n1 = sem("dv_n1")
        dv_r0 = sem("dv_r0")
        dv_n0 = sem("dv_n0")
        dv_y = sem("dv_y")
        dv_z = sem("dv_z")
        dv_st = sem("dv_st")
        dv_bn = sem("dv_bn")
        dv_out = sem("dv_out")
        po_kb0l = sem("po_kb0l")
        po_m1 = sem("po_m1")
        po_rstd = sem("po_rstd")

        fold0, fold1, negc, ident = (a.bitcast(BF16) for a in (fold0, fold1, negc, ident))
        SETUP_LOADS = 31
        BANK_MM = dict(start=True, stop=True)
        block = ctx.enter_context(nc.Block())

        def after(eng, signal, count):
            if not isinstance(count, int) or count > 0:
                eng.wait_ge(signal, count)

        @block.sync
        def _(sp):
            for dst, src in ((aqT_sb, aqT), (bq_sb, bq), (akvT_sb, akvT), (bkv_sb, bkv), (aoT_sb, aoT), (bo_sb, bo),
                             (w1q_sb, w1q), (w1k_sb, w1k), (w1v_sb, w1v), (wkv_sb, wkv), (wq_sb, wq), (wo_sb, wo),
                             (w1o_sb, w1o), (w1bias_sb, w1bias), (b1v_sb, b1v), (sel0_sb, sel0), (selq_sb, selq),
                             (selk_sb, selk), (fold0_sb, fold0), (negc_sb, negc), (ones0_sb, ones0),
                             (ident_sb, ident), (mask_sb, mask)):
                sp.dma_start(dst[:], src).then_inc(ld_w, 16)
            for k, src in enumerate((b1q, b1k, b1o)):
                sp.dma_start(b1_sb[:, k:k + 1], src).then_inc(ld_w, 16)
            for g in range(2):
                sp.dma_start(fold1_sb[:, :, g * 4:(g + 1) * 4].rearrange("p a c n h t -> p a (c n h t)"), fold1)\
                  .then_inc(ld_w, 16)
                sp.dma_start(mT1[:, g, :], negc).then_inc(ld_w, 16)
            sp.dma_start(v1b[:], ones1).then_inc(ld_w, 16)

            def load_x(j):
                sp.dma_start(xT_sb[:], xT[bass.ds(j * P, P)]).then_inc(ld_x, 16)

            def load_c(j):
                sp.dma_start(cT_sb[:], cT[bass.ds(j * P, P)]).then_inc(ld_c, 16)

            def load_cn(j):
                sp.dma_start(cn_sb[:], cn[bass.ds(j * P, P), :]).then_inc(ld_cn, 16)

            def load_rows(j):
                sp.dma_start(xn_sb[:], xn[bass.ds(j * P, P), :]).then_inc(ld_xn, 16)
                for n in range(2):
                    sp.dma_start(mk_sb[n * S:(n + 1) * S, :],
                                 mask[bass.ds(j * 2 + n, 1), :].to_broadcast([S, H])).then_inc(ld_mk, 16)

            def load_masked(j):
                for n in range(2):
                    src = masked_dram[:, bass.ds(j * 2 + n, 1), :].rearrange("p o (c t) -> p (o c) t", c=NC)
                    for hp in range(2):
                        for half in range(2):
                            sp.dma_start(fold1_sb[MROWS:MROWS + PARTS, hp, :, n, half, :], src).then_inc(ld_km, 16)

            load_cn(0)
            load_c(0)
            load_x(0)
            load_rows(0)
            sp.wait_ge(set_dve, 1)
            for k in range(PARTS):
                sp.dma_start(masked_dram[k], masked_sb[:]).then_inc(st_km, 16)
            sp.wait_ge(st_km, 16 * PARTS)
            sp.wait_ge(ld_w, 16 * SETUP_LOADS)
            load_masked(0)
            sp.wait_ge(pe_v1, 2)
            load_cn(1)

            def step(i, more, more_cn):
                if more:
                    sp.wait_ge(pe_kv0, i + 1)
                    load_c(i + 1)
                    sp.wait_ge(pe_q0, i + 1)
                    load_x(i + 1)
                    sp.wait_ge(pe_st, i * UNITS + UNITS1)
                    load_masked(i + 1)
                if more_cn:
                    sp.wait_ge(pe_v1, i * 2 + 4)
                    load_cn(i + 2)
                sp.wait_ge(dv_out, i + 1)
                sp.dma_start(out[bass.ds(i * P, P), :], res[:]).then_inc(st_out, 16)
                if more:
                    load_rows(i + 1)

            step(0, True, True)
            with sp.Fori(1, PAIRS - 2) as i:
                step(i, True, True)
            step(PAIRS - 2, True, False)
            step(PAIRS - 1, False, False)
            sp.wait_ge(st_out, 16 * PAIRS)

        @block.tensor
        def _(pe):
            mm = nc.tensor.matmul

            pe.wait_ge(ld_w, 16 * SETUP_LOADS)
            lows = [(aqT_sb[:, k, :], bq_sb[:], H) for k in range(KT)]
            lows += [(aoT_sb[:, r, :], bo_sb[:], H) for r in range(REP)]
            lows += [(akvT_sb[:, s, k, :], bkv_sb[:, s, :], P) for k in range(KT) for s in range(2)]
            for n, (a, b, w) in enumerate(lows):
                if n >= 2:
                    pe.wait_ge(set_dve, n)
                mm(PR[n % 2][:, 0:w], a, b, **BANK_MM).then_inc(set_pe, 1)
            pe.wait_ge(set_dve, len(lows))
            mm(PR[0][:, 0:1], w1bias_sb[:], b1v_sb[:], **BANK_MM).then_inc(set_pe, 1)
            pe.wait_ge(set_dve, len(lows) + 2)

            def project_qk1(j):
                pe.wait_ge(ld_cn, j * 16 + 16)
                mm(PR[0][:], w1q_sb[:], cn_sb[:], **BANK_MM).then_inc(pe_qk1, 1)
                mm(PR[1][:], w1k_sb[:], cn_sb[:], **BANK_MM).then_inc(pe_qk1, 1)

            def project_v1(j):
                for g in range(2):
                    after(pe, ac_ex, j * UNITS)
                    for c in range(4):
                        for dup in range(2):
                            last = mm(ST[g][dup * CH:(dup + 1) * CH, c * P:(c + 1) * P],
                                      cn_sb[:, (g * 4 + c) * CH:(g * 4 + c + 1) * CH], w1v_sb[:], **BANK_MM)
                    last.then_inc(pe_v1, 1)

            project_qk1(0)
            project_v1(0)

            def step(i, more):
                pe.wait_ge(ld_c, i * 16 + 16)
                after(pe, dv_n1, i * 2)
                for k in range(KT):
                    mm(PV[0][:, 0:P], wkv_sb[:, k, 0, :], cT_sb[:, k, :], start=(k == 0), stop=(k == KT - 1))
                for b in range(2):
                    for k in range(KT):
                        for dup in range(2):
                            last = mm(PV[0][dup * S:(dup + 1) * S, (b + 1) * P:(b + 2) * P],
                                      cT_sb[:, k, b * S:(b + 1) * S], wkv_sb[:, k, 1, :],
                                      start=(k == 0), stop=(k == KT - 1))
                last.then_inc(pe_kv0, 1)
                pe.wait_ge(ld_x, i * 16 + 16)
                for r in range(REP):
                    for k in range(KT):
                        last = mm(PV[1][:, r * P:(r + 1) * P], wq_sb[:, k, r, :], xT_sb[:, k, :],
                                  start=(k == 0), stop=(k == KT - 1))
                last.then_inc(pe_q0, 1)

                pe.wait_ge(ac_m1, i * 8 + 8)
                pe.wait_ge(ld_km, i * 128 + 128)
                for c in range(NC):
                    if c < 2:
                        after(pe, dv_n0, i)
                    else:
                        pe.wait_ge(dv_mx, i * UNITS + c - 1)
                    for hp in range(2):
                        o = SN[c % 2][:, hp * 256:(hp + 1) * 256]
                        mm(o, qm1h[:, c, 2 * hp:2 * hp + 2, :].rearrange("p h q -> p (h q)"),
                           kb1h[:, c].rearrange("p a t -> p (a t)"), start=True, stop=False)
                        last = mm(o, negc_sb[:], fold1_sb[:, 0, c].rearrange("p n h t -> p (n h t)"),
                                  start=False, stop=True)
                    last.then_inc(pe_sn, 1)
                pe.wait_ge(dv_kb0h, i + 1)
                pe.wait_ge(ac_q0h, i + 1)
                for u in range(UNITS0):
                    b, rp = u // 2, u % 2
                    pe.wait_ge(dv_mx, i * UNITS + UNITS1 + u - 1)
                    mm(SN[u % 2][:], q0h[:, b, 2 * rp:2 * rp + 2, :].rearrange("p r q -> p (r q)"),
                       kb0h[:, b].rearrange("p g t -> p (g t)"), **BANK_MM).then_inc(pe_sn, 1)
                if more:
                    after(pe, dv_z, i)
                    project_qk1(i + 1)

                pe.wait_ge(dv_p1, i * 5 + 5)
                pe.wait_ge(ac_v1, i * 4 + 4)
                mt = ST[1][:].bitcast(BF16)
                for g in range(2):
                    nc.tensor.transpose(mt[0:MROWS, g * P:(g + 1) * P], m1p[:, g].rearrange("p a m -> p (a m)"),
                                        ident_sb[:]).then_inc(pe_mt, 1)

                def scores1(c):
                    if c == 0:
                        pe.wait_ge(po_m1, i * 2 + 2)
                        pe.wait_ge(ac_mt, i * 3 + 2)
                    elif c > 1:
                        pe.wait_ge(ac_ex, i * UNITS + c - 1)
                    for n in range(2):
                        o = ST[c % 2][:, n * 256:(n + 1) * 256]
                        kh = kb1h[:, c, 2 * n:2 * n + 2, :].rearrange("p h t -> p (h t)")
                        kl = kb1l[:, c, 2 * n:2 * n + 2, :].rearrange("p h t -> p (h t)")
                        qh = qm1h[:, c].rearrange("p h q -> p (h q)")
                        ql = qm1l[:, c].rearrange("p h q -> p (h q)")
                        mm(o, kh, qh, start=True, stop=False)
                        mm(o, kh, ql, start=False, stop=False)
                        mm(o, kl, qh, start=False, stop=False)
                        for hp in range(2):
                            last = mm(o[:, hp * P:(hp + 1) * P],
                                      fold1_sb[:, hp, c, n].rearrange("p h t -> p (h t)"),
                                      mT1[:, c // 4, :], start=False, stop=(hp == 1))
                    last.then_inc(pe_st, 1)

                def values1(c):
                    if c == 0:
                        pe.wait_ge(ac_v0, i * 2 + 2)
                        pe.wait_ge(dv_k0l, i + 1)
                        pe.wait_ge(dv_q0l, i + 1)
                    pe.wait_ge(ac_ex, i * UNITS + c + 1)
                    for n in range(2):
                        for h in range(4):
                            last = mm(PV[c // 4][h * QD:(h + 1) * QD,
                                                 (n * 4 + c % 4) * CH:(n * 4 + c % 4 + 1) * CH],
                                      v1b[:, c, n, h, :],
                                      pT[:, c % RING, (n * 4 + h) * CH:(n * 4 + h + 1) * CH], **BANK_MM)
                    last.then_inc(pe_pv, 1)

                for c in range(NC):
                    scores1(c)
                    if c >= 1:
                        values1(c - 1)
                    if c == 2:
                        pe.wait_ge(dv_p0, i * 5 + 5)
                        nc.tensor.transpose(SN[0][:].bitcast(BF16)[0:MROWS, 0:P],
                                            m0p[:].rearrange("p a m -> p (a m)"), ident_sb[:]).then_inc(pe_mt, 1)

                def scores0(u):
                    if u == 0:
                        pe.wait_ge(ac_mt, i * 3 + 3)
                        pe.wait_ge(po_kb0l, i + 1)
                    pe.wait_ge(ac_ex, i * UNITS + UNITS1 + u - 1)
                    b = u // 2
                    qh = q0h[:, b].rearrange("p r q -> p (r q)")
                    ql = q0l[:, b].rearrange("p r q -> p (r q)")
                    for j in range(2):
                        pair = 2 * (u % 2) + j
                        o = ST[u % 2][:, j * 256:(j + 1) * 256]
                        kh = kb0h[:, b, 2 * pair:2 * pair + 2, :].rearrange("p g t -> p (g t)")
                        kl = kb0l[:, b, 2 * pair:2 * pair + 2, :].rearrange("p g t -> p (g t)")
                        mm(o, kh, qh, start=True, stop=False)
                        mm(o, kh, ql, start=False, stop=False)
                        mm(o, kl, qh, start=False, stop=False)
                        for rp in range(2):
                            last = mm(o[:, rp * P:(rp + 1) * P], fold0_sb[:, b, rp, pair, :], mT0[:],
                                      start=False, stop=(rp == 1))
                    last.then_inc(pe_st, 1)

                def values0(u):
                    pe.wait_ge(ac_ex, i * UNITS + UNITS1 + u + 1)
                    b = u // 2
                    for j in range(2):
                        pair = 2 * (u % 2) + j
                        rows = slice(pair * QD, (pair + 1) * QD)
                        pt = pT[:, u % RING, j * 256:(j + 1) * 256]
                        mm(SN[0][rows, b * 256:(b + 1) * 256], v0b[:, b, pair, :], pt, **BANK_MM)
                        last = mm(SN[1][rows, b * 256:(b + 1) * 256], ones0_sb[:], pt, **BANK_MM)
                    last.then_inc(pe_pv, 1)

                scores0(0)
                values1(NC - 1)
                for u in range(1, UNITS0):
                    scores0(u)
                    values0(u - 1)
                values0(UNITS0 - 1)

                if more:
                    pe.wait_ge(ac_qk1h, i * 2 + 4)
                    pe.wait_ge(dv_qk1l, i * 2 + 4)
                    project_v1(i + 1)
                pe.wait_ge(dv_n1, i * 2 + 2)
                for n in range(2):
                    last = mm(PR[0][n * S:(n + 1) * S, :], w1o_sb[:], o1n[:, n].rearrange("p g q -> p (g q)"),
                              **BANK_MM)
                last.then_inc(pe_o1, 1)
                pe.wait_ge(dv_n0, i + 1)
                for r in range(REP):
                    last = mm(PR[1][:], o0[:, r].rearrange("p b q -> p (b q)"), wo_sb[:, r, :],
                              start=(r == 0), stop=(r == REP - 1))
                last.then_inc(pe_o0, 1)

            step(0, True)
            with pe.Fori(1, PAIRS - 1) as i:
                step(i, True)
            step(PAIRS - 1, False)

        @block.scalar
        def _(act):
            f = nc.scalar.activation

            def high_qk1(j):
                after(act, ac_m1, j * 8)
                act.wait_ge(pe_qk1, j * 2 + 1)
                f(q1h[:], PR[0][:], ACT.Identity, bias=b1_sb[:, 0:1]).then_inc(ac_qk1h, 1)
                act.wait_ge(pe_qk1, j * 2 + 2)
                f(k1h[:], PR[1][:], ACT.Identity, bias=b1_sb[:, 1:2]).then_inc(ac_qk1h, 1)

            def mask_high1(j, a, b):
                for m in range(a, b):
                    src, dst, sel = ((q1h, qm1h, selq_sb), (k1h, kb1h, selk_sb))[m // 4]
                    act.wait_ge(ac_qk1h, j * 2 + 2)
                    f(dst[:, :, m % 4, :], src[:].bitcast(F32).rearrange("p (c q) -> p c q", c=NC), ACT.Copy,
                      scale=sel[:, m % 4:m % 4 + 1]).then_inc(ac_m1, 1)

            def copy_v1(j):
                for g in range(2):
                    act.wait_ge(pe_v1, j * 2 + g + 1)
                    for dup in range(2):
                        rows = slice(dup * CH, (dup + 1) * CH)
                        f(v1b[rows, g * 4:(g + 1) * 4, :, :, dup * HD1:(dup + 1) * HD1]
                          .rearrange("p c n h d -> p c (n h) d"),
                          ST[g][rows].rearrange("p (c u m d) -> p c u m d", c=4, u=2, d=HD1)[:, :, dup],
                          ACT.Copy).then_inc(ac_v1, 1)

            act.wait_ge(ld_w, 16 * SETUP_LOADS)
            high_qk1(0)
            mask_high1(0, 0, 8)
            copy_v1(0)

            def step(i, more):
                act.wait_ge(pe_kv0, i + 1)
                f(k0h[:].rearrange("p b t -> p (b t)"), PV[0][:, 0:P], ACT.Copy).then_inc(ac_k0h, 1)
                act.wait_ge(set_pool, 1)
                for dup in range(2):
                    rows = slice(dup * S, (dup + 1) * S)
                    f(v0b[rows, :, :, dup * HD:(dup + 1) * HD],
                      PV[0][rows, P:3 * P].rearrange("p (b m u d) -> p b m u d", b=2, m=4, u=2)[:, :, :, dup],
                      ACT.Copy).then_inc(ac_v0, 1)
                act.wait_ge(pe_q0, i + 1)
                f(q0h[:].rearrange("p b r q -> p r b q"),
                  PV[1][:].rearrange("p (r b q) -> p r b q", r=REP, b=2), ACT.Copy).then_inc(ac_q0h, 1)
                if more:
                    high_qk1(i + 1)
                mt = ST[1][:].bitcast(BF16)
                act.wait_ge(pe_mt, i * 3 + 2)
                for g in range(2):
                    f(mT1[0:MROWS, g, :], mt[0:MROWS, g * P:(g + 1) * P], ACT.Copy).then_inc(ac_mt, 1)

                def exps(u):
                    act.wait_ge(pe_st, i * UNITS + u + 1)
                    if u < RING:
                        after(act, pe_pv, i * UNITS)
                    else:
                        act.wait_ge(pe_pv, i * UNITS + u - RING + 1)
                    f(pT[:, u % RING, :], ST[u % 2][:], ACT.Exp,
                      scale=SCALE1 if u < UNITS1 else SCALE0).then_inc(ac_ex, 1)

                for u in range(UNITS1):
                    exps(u)
                    if u == 2:
                        act.wait_ge(pe_mt, i * 3 + 3)
                        f(mT0[:], SN[0][:].bitcast(BF16)[0:MROWS, 0:P], ACT.Copy).then_inc(ac_mt, 1)
                for u in range(UNITS0):
                    exps(UNITS1 + u)
                    if more and u < UNITS0 - 1:
                        mask_high1(i + 1, 2 * u, 2 * u + 2)
                if more:
                    copy_v1(i + 1)
                    mask_high1(i + 1, 6, 8)

            step(0, True)
            with act.Fori(1, PAIRS - 1) as i:
                step(i, True)
            step(PAIRS - 1, False)

        @block.gpsimd
        def _(pool):
            nc.gpsimd.memset(v0b[:], 0.0).then_inc(set_pool, 1)
            nc.gpsimd.memset(minus_half[:], -0.5).then_inc(set_pool, 1)
            pool.wait_ge(set_pool, 2)

            def mask_low1(j):
                pool.wait_ge(dv_qk1l, j * 2 + 2)
                for src, dst, sel in ((q1l, qm1l, selq_sb), (k1l, kb1l, selk_sb)):
                    nc.gpsimd.tensor_tensor(
                        dst[:], src[:].bitcast(F32).rearrange("p (c q) -> p c q", c=NC).unsqueeze(2)
                        .to_broadcast([P, NC, 4, CH]),
                        sel[:].unsqueeze(1).unsqueeze(3).to_broadcast([P, NC, 4, CH]), ALU.mult).then_inc(po_m1, 1)

            pool.wait_ge(ld_w, 16 * SETUP_LOADS)
            mask_low1(0)

            def step(i, more):
                pool.wait_ge(dv_k0l, i + 1)
                nc.gpsimd.tensor_tensor(
                    kb0l[:], k0l[:].bitcast(F32).unsqueeze(2).to_broadcast([P, 2, NKV, S]),
                    sel0_sb[:].unsqueeze(1).unsqueeze(3).to_broadcast([P, 2, NKV, S]), ALU.mult).then_inc(po_kb0l, 1)
                if more:
                    pool.wait_ge(pe_st, i * UNITS + UNITS1)
                    mask_low1(i + 1)
                pool.wait_ge(dv_st, i * 3 + 3)
                nc.gpsimd.tensor_tensor(rstd[:], vare[:], minus_half[:], ALU.pow).then_inc(po_rstd, 1)

            step(0, True)
            with pool.Fori(1, PAIRS - 1) as i:
                step(i, True)
            step(PAIRS - 1, False)

        @block.vector
        def _(dve):
            v = nc.vector

            dve.wait_ge(ld_w, 16 * SETUP_LOADS)
            v.tensor_scalar(masked_sb[:], mask_sb[:], 0.0, None, ALU.is_le).then_inc(set_dve, 1)
            whole = [wq_sb[:, k].rearrange("p r m -> p (r m)") for k in range(KT)]
            whole += [wo_sb[:, r, :] for r in range(REP)]
            whole += [wkv_sb[:, k, s, :] for k in range(KT) for s in range(2)]
            for n, w in enumerate(whole):
                dve.wait_ge(set_pe, n + 1)
                cols = H if n < KT + REP else P
                v.scalar_tensor_tensor(out=w, in0=PR[n % 2][:, 0:cols], scalar=LORA, in1=w, op0=ALU.mult,
                                       op1=ALU.add).then_inc(set_dve, 1)
            dve.wait_ge(set_pe, len(whole) + 1)
            v.tensor_tensor(b1_sb[:, 3:4], PR[0][:, 0:1], b1_sb[:, 2:3], ALU.add).then_inc(set_dve, 1)

            def low_qk1(j):
                after(dve, po_m1, j * 2)
                for m, (hi, lo) in enumerate(((q1h, q1l), (k1h, k1l))):
                    dve.wait_ge(ac_qk1h, j * 2 + m + 1)
                    v.scalar_tensor_tensor(out=lo[:], in0=PR[m][:], scalar=b1_sb[:, m:m + 1],
                                           in1=hi[:].bitcast(F32), op0=ALU.add,
                                           op1=ALU.subtract).then_inc(dv_qk1l, 1)

            low_qk1(0)

            def alone():
                dve.wait_ge(ld_w, 16 * SETUP_LOADS)

            def split3(m, p, r, done, at):
                v.tensor_copy(p[0], m).then_inc(done, 1)
                dve.wait_ge(done, at + 1)
                v.tensor_tensor(r[0], m, p[0], ALU.subtract).then_inc(done, 1)
                dve.wait_ge(done, at + 2)
                v.tensor_copy(p[1], r[0]).then_inc(done, 1)
                dve.wait_ge(done, at + 3)
                v.tensor_tensor(r[1], r[0], p[1], ALU.subtract).then_inc(done, 1)
                dve.wait_ge(done, at + 4)
                v.tensor_copy(p[2], r[1]).then_inc(done, 1)

            def step(i, more):
                dve.wait_ge(ac_k0h, i + 1)
                dve.wait_ge(ac_v0, i * 2 + 2)
                after(dve, po_kb0l, i)
                v.tensor_tensor(k0l[:].rearrange("p b t -> p (b t)"), PV[0][:, 0:P],
                                k0h[:].bitcast(F32).rearrange("p b t -> p (b t)"),
                                ALU.subtract).then_inc(dv_k0l, 1)
                v.tensor_tensor(kb0h[:], k0h[:].bitcast(F32).unsqueeze(2).to_broadcast([P, 2, NKV, S]),
                                sel0_sb[:].unsqueeze(1).unsqueeze(3).to_broadcast([P, 2, NKV, S]),
                                ALU.mult).then_inc(dv_kb0h, 1)
                for u in range(UNITS1):
                    dve.wait_ge(pe_sn, i * UNITS + u + 1)
                    v.tensor_reduce(m1[:, u // 4, (u % 4) * 8:(u % 4) * 8 + 8],
                                    SN[u % 2][:].rearrange("p (m t) -> p m t", t=CH), AX_X,
                                    ALU.max).then_inc(dv_mx, 1)
                    if u == 1:
                        dve.wait_ge(ac_q0h, i + 1)
                        v.tensor_tensor(q0l[:].rearrange("p b r q -> p r b q"),
                                        PV[1][:].rearrange("p (r b q) -> p r b q", r=REP, b=2),
                                        q0h[:].bitcast(F32).rearrange("p b r q -> p r b q"),
                                        ALU.subtract).then_inc(dv_q0l, 1)
                dve.wait_ge(dv_mx, i * UNITS + UNITS1)
                split3(m1[:], [m1p[:, :, k, :] for k in range(PARTS)], [m1r[:, k] for k in range(2)], dv_p1,
                       i * 5)
                for u in range(UNITS0):
                    dve.wait_ge(pe_sn, i * UNITS + UNITS1 + u + 1)
                    v.tensor_reduce(m0[:, u * NKV:(u + 1) * NKV],
                                    SN[u % 2][:].rearrange("p (m t) -> p m t", t=S), AX_X,
                                    ALU.max).then_inc(dv_mx, 1)
                dve.wait_ge(dv_mx, i * UNITS + UNITS)
                split3(m0[:], [m0p[:, k, :] for k in range(PARTS)], [m0r[:, k] for k in range(2)], dv_p0,
                       i * 5)
                if more:
                    low_qk1(i + 1)

                for g in range(2):
                    alone()
                    dve.wait_ge(pe_pv, i * UNITS + 4 * g + 4)
                    v.stream_shuffle(sum1[:], PV[g][:], [j % 16 + 16 for j in range(32)]).then_inc(dv_s1, 1)
                    dve.wait_ge(dv_s1, i * 2 + g + 1)
                    v.reciprocal(rec1[:], sum1[:]).then_inc(dv_r1, 1)
                    dve.wait_ge(dv_r1, i * 2 + g + 1)
                    v.tensor_tensor(o1n[:, :, g, :], PV[g][:].rearrange("p (n q) -> p n q", n=2),
                                    rec1[:].rearrange("p (n q) -> p n q", n=2), ALU.mult).then_inc(dv_n1, 1)
                dve.wait_ge(pe_pv, i * UNITS + UNITS)
                v.reciprocal(rec0[:], SN[1][:]).then_inc(dv_r0, 1)
                dve.wait_ge(dv_r0, i + 1)
                v.tensor_tensor(o0[:].rearrange("p r b q -> p b r q"),
                                SN[0][:].rearrange("p (b r q) -> p b r q", b=2, r=REP),
                                rec0[:].rearrange("p (b r q) -> p b r q", b=2, r=REP),
                                ALU.mult).then_inc(dv_n0, 1)

                dve.wait_ge(pe_o1, i + 1)
                dve.wait_ge(ld_mk, i * 32 + 32)
                v.scalar_tensor_tensor(out=y1[:], in0=PR[0][:], scalar=b1_sb[:, 3:4], in1=mk_sb[:], op0=ALU.add,
                                       op1=ALU.mult).then_inc(dv_y, 1)
                dve.wait_ge(ld_xn, i * 16 + 16)
                dve.wait_ge(dv_y, i + 1)
                v.tensor_tensor(y1[:], y1[:], xn_sb[:], ALU.add).then_inc(dv_st, 1)
                dve.wait_ge(dv_st, i * 3 + 1)
                dve.wait_ge(pe_o0, i + 1)
                v.tensor_tensor(z[:], PR[1][:], y1[:], ALU.add).then_inc(dv_z, 1)
                dve.wait_ge(dv_z, i + 1)
                v.bn_stats(stats[:], z[:]).then_inc(dv_bn, 1)
                alone()
                dve.wait_ge(dv_bn, i + 1)
                v.bn_aggr(mv[:], stats[:]).then_inc(dv_st, 1)
                dve.wait_ge(dv_st, i * 3 + 2)
                v.tensor_scalar(vare[:], mv[:, 1:2], EPS, None, ALU.add).then_inc(dv_st, 1)
                dve.wait_ge(po_rstd, i + 1)
                after(dve, st_out, i * 16)
                v.tensor_scalar(res[:], z[:], mv[:, 0:1], rstd[:, 0:1], ALU.subtract,
                                ALU.mult).then_inc(dv_out, 1)

            step(0, True)
            with dve.Fori(1, PAIRS - 1) as i:
                step(i, True)
            step(PAIRS - 1, False)


def lay_out(inp):
    import numpy as np

    def bf16(a):
        return (np.asarray(a, np.float32).view(np.uint32) >> 16).astype(np.uint16)

    x, c = np.asarray(inp["x"]), np.asarray(inp["ctx_4096"])

    def turned(a):
        return np.ascontiguousarray(a.reshape(PAIRS, P, KT, P).transpose(0, 3, 2, 1)).reshape(PAIRS * P, KT, P)

    def by_r(a, axis):
        s = a.shape
        a = a.reshape(s[:axis] + (NKV, REP, HD) + s[axis + 1:])
        return np.swapaxes(a, axis, axis + 1).reshape(s)

    g = {k[9:]: np.asarray(v) for k, v in inp.items() if k.startswith("L0_xattn_") or k.startswith("L1_xattn_")}
    out = {
        "xT": turned(x), "xn": x.reshape(N * S, H), "cT": turned(c), "cn": c.reshape(N * S, H),
        "mask": np.asarray(inp["mask_Bx1x4096_ff1"]).reshape(N, H),
        "wq": by_r(g["Wq"], 1).reshape(KT, P, REP, P).transpose(1, 0, 2, 3),
        "aqT": g["Aq"].T.reshape(R, KT, P), "bq": by_r(g["Bq"], 1),
        "wkv": np.stack([g["Wk"], g["Wv"]], 1).reshape(KT, P, 2, P).transpose(1, 0, 2, 3),
        "akvT": np.stack([g["Ak"].T, g["Av"].T], 1).reshape(R, 2, KT, P), "bkv": np.stack([g["Bk"], g["Bv"]], 1),
        "wo": by_r(g["Wo"], 0).reshape(REP, P, H).transpose(1, 0, 2),
        "aoT": by_r(g["Ao"], 0).T.reshape(R, REP, P), "bo": g["Bo"],
    }
    win, bin_, wout, bout = g["W_in"], g["b_in"], g["W_out"], g["b_out"]
    C = 64
    for k, name in enumerate(("w1q", "w1k", "w1v")):
        w = win[k * C:(k + 1) * C]
        both = np.zeros((2, C, 2, C), np.float32)
        for n in range(2):
            both[n, :, n, :] = w.T
        if name == "w1v":
            both = both.reshape(2, C, 2, 2, 4 * HD1).transpose(0, 1, 3, 2, 4)
        out[name] = both.reshape(P, P)
    out["b1q"] = np.tile(bin_[0:C], 2).reshape(P, 1)
    out["b1k"] = np.tile(bin_[C:2 * C], 2).reshape(P, 1)
    out["b1v"] = bin_[2 * C:].reshape(C, 1)
    out["b1o"] = np.tile(bout, 2).reshape(P, 1)
    out["w1bias"] = np.concatenate([wout.T, wout.T], 1)
    w1o = np.zeros((4, QD, C), np.float32)
    w1o[:, 0:16] = wout.T.reshape(2, 4, HD1, C).transpose(1, 0, 2, 3).reshape(4, 16, C)
    out["w1o"] = w1o.reshape(P, C)

    rows = np.arange(P)
    out["sel0"] = (rows[:, None] // HD == np.arange(NKV)).astype(np.float32)
    out["selq"] = (rows[:, None] // HD1 % 4 == np.arange(4)).astype(np.float32)
    out["selk"] = (rows[:, None] // 32 == np.arange(4)).astype(np.float32)
    f0 = np.zeros((PARTS, 2, 2, NKV, 2, 2, 4, 2, S), np.float32)
    for b in range(2):
        for rp in range(2):
            for h in range(NKV):
                f0[:, b, rp, h, b, rp, h // 2, h % 2, :] = -1
    out["fold0"] = bf16(f0.reshape(MROWS, 2, 2, 4, P))
    f1 = np.zeros((PARTS, 4, 2, 2, 2, 2, 4, 2, 2, CH), np.float32)
    for c4 in range(4):
        for hp in range(2):
            for n in range(2):
                for half in range(2):
                    f1[:, c4, hp, n, half, hp, c4, n, half, :] = -1
    fold1 = np.zeros((P, 2, 4 * 2 * 2 * CH), np.float32)
    fold1[0:MROWS] = f1.reshape(MROWS, 2, 4 * 2 * 2 * CH)
    out["fold1"] = bf16(fold1)
    neg = np.full(P, -1e9 / SCALE1, np.float32)
    negc = np.zeros((P, P), np.float32)
    for k in range(PARTS):
        negc[MROWS + k] = (neg.view(np.uint32) & 0xFFFF0000).view(np.float32)
        neg = neg - negc[MROWS + k]
    out["negc"] = bf16(negc)
    out["ones0"] = np.repeat((rows[:, None] // S == np.arange(2)).astype(np.float32), HD, 1)
    o1 = np.zeros((2, CH, NC, 2, 4, 2, 2, HD1), np.float32)
    for half in range(2):
        o1[half, :, :, :, :, 1, half, :] = 1
    out["ones1"] = o1.reshape(P, NC, 2, 4, QD)
    out["ident"] = bf16(np.eye(P))
    return {k: np.ascontiguousarray(v) for k, v in out.items()}


def kernel(**inputs):
    import concourse.bacc as _bacc
    from concourse.bass_utils import run_bass_kernel_spmd as _run

    nc = _bacc.Bacc("TRN2", target_bir_lowering=False, num_devices=1)
    arrays = lay_out(inputs)
    args = {k: nc.dram_tensor(f"in_{k}", a.shape, mybir.dt.from_np(a.dtype), kind="ExternalInput").ap()
            for k, a in arrays.items()}
    out = nc.dram_tensor("out", (N * S, H), F32, kind="ExternalOutput").ap()
    build(nc, out=out, **args)
    r = _run(nc, [{f"in_{k}": a for k, a in arrays.items()}], core_ids=[0])
    return r.results[0]["out"].reshape(N, S, H)
```

```python
from contextlib import ExitStack

import concourse.bass as bass
from concourse import mybir

F32 = mybir.dt.float32
F32R = mybir.dt.float32r
BF16 = mybir.dt.bfloat16
ACT = mybir.ActivationFunctionType
ALU = mybir.AluOpType
AX_X = mybir.AxisListType.X

N, S, H = 32, 64, 512
PAIRS = N // 2
P = 128
KT = H // P
NKV, REP, HD = 8, 4, 16
R = 16
CH, NC, NH1, HD1 = 64, 8, 8, 8
QD = 32
SCALE0 = HD ** -0.5
SCALE1 = HD1 ** -0.5
LORA = 2.0
EPS = 1e-5
PARTS = 3
MROWS = 32 * PARTS
UNITS1, UNITS0 = NC, 4
UNITS = UNITS1 + UNITS0
RING = 4
LOWS = 16
LOW = LOWS * P + 2 * P + 2 * H
CONSTS = 20 + QD + S


def low_factors(t, n):
    a = t[:, n * P:(n + 1) * P]
    right = LOWS * P
    if n < 2 * KT:
        return a, t[:, right + (n % 2) * P:right + (n % 2 + 1) * P], P
    right += 2 * P + (0 if n < 3 * KT else H)
    return a, t[:, right:right + H], H


def build(nc, xT, xn, cT, cn, mask, wq, wkv, wo, low, w1, consts, folds, fold1, ones1, b1v, w1bias, out):
    with ExitStack() as ctx:
        def sb(name, shape, dt=F32):
            return ctx.enter_context(nc.sbuf_tensor(name, shape, dt))

        def ps(name, dt=F32):
            return ctx.enter_context(nc.psum_tensor(name, [P, H], dt))

        def sem(name):
            return ctx.enter_context(nc.semaphore(name))

        masked_dram = nc.dram_tensor("masked_rows", (PAIRS, 2 * NC, 2, 2 * CH), BF16, kind="Internal").ap()

        wq_sb = sb("wq_sb", [P, KT, REP, P])
        wkv_sb = sb("wkv_sb", [P, KT, 2, P])
        wo_sb = sb("wo_sb", [P, REP, H])
        woh = sb("woh", [P, REP, H], F32R)
        wol = sb("wol", [P, REP, H], F32R)
        low_sb = sb("low_sb", [P, LOW])
        w1_sb = sb("w1_sb", [P, 3, P])
        consts_sb = sb("consts_sb", [P, CONSTS])
        b1v_sb = sb("b1v_sb", [S, 1])
        w1bias_sb = sb("w1bias_sb", [S, P])
        b1_sb = consts_sb[:, 0:4]
        sel0_sb = consts_sb[:, 4:12]
        selq_sb = consts_sb[:, 12:16]
        selk_sb = consts_sb[:, 16:20]
        ones0_sb = consts_sb[:, 20:20 + QD]
        w1o_sb = consts_sb[:, 20 + QD:20 + QD + S]
        folds_sb = sb("folds_sb", [P, 18, P], BF16)
        fold0_sb = folds_sb[0:MROWS, 0:16, :].rearrange("p (b r m) n -> p b r m n", b=2, r=2)
        negc_sb = folds_sb[:, 16, :]
        ident_sb = folds_sb[:, 17, :]
        fold1_sb = sb("fold1_sb", [P, 2, NC, 2, 2, CH], BF16)
        mask_sb = sb("mask_sb", [N, H])
        masked_sb = sb("masked_sb", [N, 2, NC, 2, CH], BF16)

        xT_sb = sb("xT_sb", [P, KT, P])
        cT_sb = sb("cT_sb", [P, KT, P])
        xn_sb = sb("xn_sb", [P, H])
        cn_sb = sb("cn_sb", [P, H])
        mk_sb = sb("mk_sb", [P, H])

        q0h = sb("q0h", [P, 2, REP, S], F32R)
        q0l = sb("q0l", [P, 2, REP, S], F32R)
        k0h = sb("k0h", [P, 2, S], F32R)
        k0l = sb("k0l", [P, 2, S], F32R)
        kb0h = sb("kb0h", [P, 2, NKV, S], F32R)
        kb0l = sb("kb0l", [P, 2, NKV, S], F32R)
        v0b = sb("v0b", [P, 2, 4, QD])
        m0 = sb("m0", [P, 32])
        m0p = sb("m0p", [P, PARTS, 32], BF16)
        m0r = sb("m0r", [P, 2, 32])
        mT0 = sb("mT0", [MROWS, P], BF16)
        rec0 = sb("rec0", [P, H])
        o0 = sb("o0", [P, REP, 2, S])
        o0h = sb("o0h", [P, REP, 2, S], F32R)
        o0l = sb("o0l", [P, REP, 2, S], F32R)

        q1h = sb("q1h", [P, H], F32R)
        q1l = sb("q1l", [P, H], F32R)
        k1h = sb("k1h", [P, H], F32R)
        k1l = sb("k1l", [P, H], F32R)
        qm1h = sb("qm1h", [P, NC, 4, CH], F32R)
        qm1l = sb("qm1l", [P, NC, 4, CH], F32R)
        kb1h = sb("kb1h", [P, NC, 4, CH], F32R)
        kb1l = sb("kb1l", [P, NC, 4, CH], F32R)
        v1b = sb("v1b", [P, NC, 2, 4, QD])
        m1 = sb("m1", [P, 2, 32])
        m1p = sb("m1p", [P, 2, PARTS, 32], BF16)
        m1r = sb("m1r", [P, 2, 2, 32])
        mT1 = sb("mT1", [P, 2, P], BF16)
        sum1 = sb("sum1", [P, H])
        rec1 = sb("rec1", [P, H])
        o1n = sb("o1n", [P, 2, 2, 4 * CH])

        pT = sb("pT", [P, RING, H])

        y1 = sb("y1", [P, H])
        y = sb("y", [P, H])
        z = sb("z", [P, H])
        stats = sb("stats", [P, 6])
        mv = sb("mv", [P, 2])
        vare = sb("vare", [P, 1])
        minus_half = sb("minus_half", [P, 1])
        rstd = sb("rstd", [P, 1])
        res = sb("res", [P, H])

        SN = [ps("sn0"), ps("sn1")]
        ST = [ps("st0"), ps("st1")]
        PR = [ps("pr0"), ps("pr1")]
        PV = [ps("pv0"), ps("pv1")]

        ld_first = sem("ld_first")
        ld_wkv = sem("ld_wkv")
        ld_wq = sem("ld_wq")
        ld_wo = sem("ld_wo")
        ld_mask = sem("ld_mask")
        ld_fold = sem("ld_fold")
        ld_v1b = sem("ld_v1b")
        ld_bias = sem("ld_bias")
        ld_x = sem("ld_x")
        ld_c = sem("ld_c")
        ld_cn = sem("ld_cn")
        ld_xn = sem("ld_xn")
        ld_mk = sem("ld_mk")
        ld_km = sem("ld_km")
        st_km = sem("st_km")
        st_out = sem("st_out")
        set_mask = sem("set_mask")
        set_w = sem("set_w")
        set_bias = sem("set_bias")
        set_wo = sem("set_wo")
        set_pool = sem("set_pool")
        set_low = sem("set_low")
        pe_kv0 = sem("pe_kv0")
        pe_q0 = sem("pe_q0")
        pe_sn = sem("pe_sn")
        pe_qk1 = sem("pe_qk1")
        pe_v1 = sem("pe_v1")
        pe_mt = sem("pe_mt")
        pe_st = sem("pe_st")
        pe_pv = sem("pe_pv")
        pe_o1 = sem("pe_o1")
        pe_o0 = sem("pe_o0")
        ac_q0h = sem("ac_q0h")
        ac_k0h = sem("ac_k0h")
        ac_v0 = sem("ac_v0")
        ac_qk1h = sem("ac_qk1h")
        ac_mt = sem("ac_mt")
        ac_ex = sem("ac_ex")
        ac_v1 = sem("ac_v1")
        ac_m1 = sem("ac_m1")
        ac_o0h = sem("ac_o0h")
        dv_q0l = sem("dv_q0l")
        dv_k0l = sem("dv_k0l")
        dv_mx = sem("dv_mx")
        dv_p1 = sem("dv_p1")
        dv_p0 = sem("dv_p0")
        dv_qk1l = sem("dv_qk1l")
        dv_s1 = sem("dv_s1")
        dv_r1 = sem("dv_r1")
        dv_n1 = sem("dv_n1")
        dv_r0 = sem("dv_r0")
        dv_n0 = sem("dv_n0")
        dv_y = sem("dv_y")
        dv_z = sem("dv_z")
        dv_bn = sem("dv_bn")
        dv_st = sem("dv_st")
        dv_out = sem("dv_out")
        po_kb0 = sem("po_kb0")
        po_m1 = sem("po_m1")
        po_y = sem("po_y")
        po_o0l = sem("po_o0l")
        po_rstd = sem("po_rstd")

        fold1, folds = (a.bitcast(BF16) for a in (fold1, folds))
        BANK_MM = dict(start=True, stop=True)
        block = ctx.enter_context(nc.Block())

        def after(eng, signal, count):
            if not isinstance(count, int) or count > 0:
                eng.wait_ge(signal, count)

        @block.sync
        def _(sp):
            def load_x(j):
                sp.dma_start(xT_sb[:], xT[bass.ds(j * P, P)]).then_inc(ld_x, 16)

            def load_c(j):
                sp.dma_start(cT_sb[:], cT[bass.ds(j * P, P)]).then_inc(ld_c, 16)

            def load_cn(j):
                sp.dma_start(cn_sb[:], cn[bass.ds(j * P, P), :]).then_inc(ld_cn, 16)

            def load_rows(j):
                sp.dma_start(xn_sb[:], xn[bass.ds(j * P, P), :]).then_inc(ld_xn, 16)
                for n in range(2):
                    sp.dma_start(mk_sb[n * S:(n + 1) * S, :],
                                 mask[bass.ds(j * 2 + n, 1), :].to_broadcast([S, H])).then_inc(ld_mk, 16)

            def load_masked(j):
                sp.dma_start(fold1_sb[MROWS:MROWS + PARTS].rearrange("p a c n h t -> p (a c n h t)"),
                             masked_dram[bass.ds(j, 1)].rearrange("o a n k -> o (a n k)")
                             .to_broadcast([PARTS, 4 * NC * 2 * CH])).then_inc(ld_km, 16)

            for n in range(2):
                sp.dma_start(mask_sb[n * PAIRS:(n + 1) * PAIRS],
                             mask.rearrange("(j n) h -> n j h", n=2)[n]).then_inc(ld_mask, 16)
            load_cn(0)
            sp.dma_start(w1_sb[:], w1).then_inc(ld_first, 16)
            sp.dma_start(consts_sb[:], consts).then_inc(ld_first, 16)
            for hp in range(2):
                for g in range(2):
                    sp.dma_start(fold1_sb[:, hp, g * 4:(g + 1) * 4].rearrange("p c n h t -> p (c n h t)"),
                                 fold1[:, hp]).then_inc(ld_fold, 16)
            for g in range(2):
                sp.dma_start(mT1[:, g, :], folds[:, 16, :]).then_inc(ld_fold, 16)
            sp.dma_start(w1bias_sb[:], w1bias).then_inc(ld_bias, 16)
            sp.dma_start(b1v_sb[:], b1v).then_inc(ld_bias, 16)
            sp.wait_ge(set_mask, 2)
            for n in range(2):
                sp.dma_start(masked_dram[:, :, n, :], masked_sb[n * PAIRS:(n + 1) * PAIRS]
                             .rearrange("p a c h t -> p (a c) (h t)")).then_inc(st_km, 16)
            load_c(0)
            sp.wait_ge(st_km, 16 * 2)
            sp.wait_ge(ld_fold, 16 * 7)
            load_masked(0)
            load_x(0)
            sp.wait_ge(pe_v1, 1)
            load_cn(1)
            load_rows(0)

            def step(i, more, more_cn):
                if more:
                    sp.wait_ge(pe_kv0, i + 1)
                    load_c(i + 1)
                after(sp, dv_out, i)
                if not isinstance(i, int) or i > 0:
                    sp.dma_start(out[bass.ds((i - 1) * P, P), :], res[:]).then_inc(st_out, 16)
                    load_rows(i)
                if more:
                    sp.wait_ge(pe_q0, i + 1)
                    load_x(i + 1)
                    sp.wait_ge(pe_st, i * UNITS + UNITS1)
                    load_masked(i + 1)
                if more_cn:
                    sp.wait_ge(pe_v1, i + 2)
                    load_cn(i + 2)

            step(0, True, True)
            with sp.Fori(1, PAIRS - 2) as i:
                step(i, True, True)
            step(PAIRS - 2, True, False)
            step(PAIRS - 1, False, False)
            sp.wait_ge(dv_out, PAIRS)
            sp.dma_start(out[(PAIRS - 1) * P:PAIRS * P, :], res[:]).then_inc(st_out, 16)
            sp.wait_ge(st_out, 16 * PAIRS)

        @block.tensor
        def _(pe):
            mm = nc.tensor.matmul

            def project_q1(j):
                pe.wait_ge(ld_cn, j * 16 + 16)
                mm(PR[0][:], w1_sb[:, 0], cn_sb[:], **BANK_MM).then_inc(pe_qk1, 1)

            def project_k1():
                mm(PR[1][:], w1_sb[:, 1], cn_sb[:], **BANK_MM).then_inc(pe_qk1, 1)

            def project_v1(j):
                after(pe, ac_ex, j * UNITS - 1)
                for c in range(NC):
                    for dup in range(2):
                        last = mm(ST[0][dup * CH:(dup + 1) * CH, c * S:(c + 1) * S],
                                  cn_sb[:, c * CH:(c + 1) * CH], w1_sb[:, 2, dup * S:(dup + 1) * S], **BANK_MM)
                last.then_inc(pe_v1, 1)

            pe.wait_ge(ld_first, 16 * 2)
            project_q1(0)
            project_k1()
            project_v1(0)

            banks = SN
            pe.wait_ge(set_low, 16)
            for n in range(LOWS):
                a, b, w = low_factors(low_sb, n)
                if n >= 2:
                    pe.wait_ge(set_w, n - 1)
                mm(banks[n % 2][:, 0:w], a, b, **BANK_MM).then_inc(set_bias, 1)
            pe.wait_ge(ld_bias, 16 * 2)
            mm(PV[0][:, 0:1], w1bias_sb[:], b1v_sb[:], **BANK_MM).then_inc(set_bias, 1)
            pe.wait_ge(set_w, LOWS + 1)
            pe.wait_ge(ld_fold, 16 * 7)

            def step(i, first, more):
                def maxima1(c):
                    if c < 2:
                        after(pe, dv_n0, i)
                    else:
                        pe.wait_ge(dv_mx, i * UNITS + c - 1)
                    for hp in range(2):
                        o = SN[c % 2][:, hp * 256:(hp + 1) * 256]
                        mm(o, qm1h[:, c, 2 * hp:2 * hp + 2, :].rearrange("p h q -> p (h q)"),
                           kb1h[:, c].rearrange("p a t -> p (a t)"), start=True, stop=False)
                        last = mm(o, negc_sb, fold1_sb[:, 0, c].rearrange("p n h t -> p (n h t)"),
                                  start=False, stop=True)
                    last.then_inc(pe_sn, 1)

                def maxima0(u):
                    b, rp = u // 2, u % 2
                    pe.wait_ge(dv_mx, i * UNITS + UNITS1 + u - 1)
                    mm(SN[u % 2][:], q0h[:, b, 2 * rp:2 * rp + 2, :].rearrange("p r q -> p (r q)"),
                       kb0h[:, b].rearrange("p g t -> p (g t)"), **BANK_MM).then_inc(pe_sn, 1)

                def project_q0(r):
                    for k in range(KT):
                        last = mm(PV[1][:, r * P:(r + 1) * P], wq_sb[:, k, r, :], xT_sb[:, k, :],
                                  start=(k == 0), stop=(k == KT - 1))
                    if r == REP - 1:
                        last.then_inc(pe_q0, 1)

                pe.wait_ge(ld_c, i * 16 + 16)
                after(pe, dv_n1, i * 2)
                for k in range(KT):
                    mm(PV[0][:, 0:P], wkv_sb[:, k, 0, :], cT_sb[:, k, :], start=(k == 0), stop=(k == KT - 1))
                for b in range(2):
                    for k in range(KT):
                        for dup in range(2):
                            last = mm(PV[0][dup * S:(dup + 1) * S, P + b * S:P + (b + 1) * S],
                                      cT_sb[:, k, b * S:(b + 1) * S], wkv_sb[:, k, 1, dup * S:(dup + 1) * S],
                                      start=(k == 0), stop=(k == KT - 1))
                last.then_inc(pe_kv0, 1)
                if not first:
                    outputs1(i - 1)
                pe.wait_ge(ld_x, i * 16 + 16)
                project_q0(0)
                pe.wait_ge(ac_m1, i * 16 + 8)
                pe.wait_ge(ld_km, i * 16 + 16)
                maxima1(0)
                maxima1(1)
                project_q0(1)
                maxima1(2)
                if not first:
                    outputs0(i - 1, 0)
                maxima1(3)
                if not first:
                    outputs0(i - 1, 1)
                pe.wait_ge(ac_m1, i * 16 + 16)
                maxima1(4)
                project_q0(2)
                maxima1(5)
                maxima1(6)
                project_q0(3)
                maxima1(7)
                if more:
                    after(pe, dv_z, i)
                    project_q1(i + 1)
                pe.wait_ge(po_kb0, i * 2 + 1)
                pe.wait_ge(ac_q0h, i + 1)
                maxima0(0)
                if more:
                    project_k1()
                maxima0(1)

                pe.wait_ge(dv_p1, i * 5 + 5)
                mt = ST[1][:].bitcast(BF16)
                for g in range(2):
                    nc.tensor.transpose(mt[0:MROWS, g * P:(g + 1) * P], m1p[:, g].rearrange("p a m -> p (a m)"),
                                        ident_sb).then_inc(pe_mt, 1)
                maxima0(2)

                def scores1(c):
                    if c == 0:
                        pe.wait_ge(po_m1, i * 2 + 2)
                        pe.wait_ge(ac_mt, i * 3 + 2)
                        pe.wait_ge(ac_v1, i * 2 + 2)
                    elif c > 1:
                        pe.wait_ge(ac_ex, i * UNITS + c - 1)
                    for n in range(2):
                        o = ST[c % 2][:, n * 256:(n + 1) * 256]
                        kh = kb1h[:, c, 2 * n:2 * n + 2, :].rearrange("p h t -> p (h t)")
                        kl = kb1l[:, c, 2 * n:2 * n + 2, :].rearrange("p h t -> p (h t)")
                        qh = qm1h[:, c].rearrange("p h q -> p (h q)")
                        ql = qm1l[:, c].rearrange("p h q -> p (h q)")
                        mm(o, kh, qh, start=True, stop=False)
                        mm(o, kh, ql, start=False, stop=False)
                        mm(o, kl, qh, start=False, stop=False)
                        for hp in range(2):
                            last = mm(o[:, hp * P:(hp + 1) * P],
                                      fold1_sb[:, hp, c, n].rearrange("p h t -> p (h t)"),
                                      mT1[:, c // 4, :], start=False, stop=(hp == 1))
                    last.then_inc(pe_st, 1)

                def values1(c):
                    if c == 0:
                        pe.wait_ge(ac_v0, i * 2 + 2)
                        pe.wait_ge(dv_k0l, i + 1)
                        pe.wait_ge(dv_q0l, i + 1)
                    pe.wait_ge(ac_ex, i * UNITS + c + 1)
                    for n in range(2):
                        for h in range(4):
                            last = mm(PV[c // 4][h * QD:(h + 1) * QD,
                                                 (n * 4 + c % 4) * CH:(n * 4 + c % 4 + 1) * CH],
                                      v1b[:, c, n, h, :],
                                      pT[:, c % RING, (n * 4 + h) * CH:(n * 4 + h + 1) * CH], **BANK_MM)
                    last.then_inc(pe_pv, 1)

                for c in range(NC):
                    scores1(c)
                    if c == 0:
                        maxima0(3)
                    if c >= 1:
                        values1(c - 1)
                    if c == 2:
                        pe.wait_ge(dv_p0, i * 5 + 5)
                        nc.tensor.transpose(SN[0][:].bitcast(BF16)[0:MROWS, 0:P],
                                            m0p[:].rearrange("p a m -> p (a m)"), ident_sb).then_inc(pe_mt, 1)

                def scores0(u):
                    if u == 0:
                        pe.wait_ge(ac_mt, i * 3 + 3)
                        pe.wait_ge(po_kb0, i * 2 + 2)
                    pe.wait_ge(ac_ex, i * UNITS + UNITS1 + u - 1)
                    b = u // 2
                    qh = q0h[:, b].rearrange("p r q -> p (r q)")
                    ql = q0l[:, b].rearrange("p r q -> p (r q)")
                    for j in range(2):
                        pair = 2 * (u % 2) + j
                        o = ST[u % 2][:, j * 256:(j + 1) * 256]
                        kh = kb0h[:, b, 2 * pair:2 * pair + 2, :].rearrange("p g t -> p (g t)")
                        kl = kb0l[:, b, 2 * pair:2 * pair + 2, :].rearrange("p g t -> p (g t)")
                        mm(o, kh, qh, start=True, stop=False)
                        mm(o, kh, ql, start=False, stop=False)
                        mm(o, kl, qh, start=False, stop=False)
                        for rp in range(2):
                            last = mm(o[:, rp * P:(rp + 1) * P], fold0_sb[:, b, rp, pair, :], mT0[:],
                                      start=False, stop=(rp == 1))
                    last.then_inc(pe_st, 1)

                def values0(u):
                    pe.wait_ge(ac_ex, i * UNITS + UNITS1 + u + 1)
                    b = u // 2
                    for j in range(2):
                        pair = 2 * (u % 2) + j
                        rows = slice(pair * QD, (pair + 1) * QD)
                        pt = pT[:, u % RING, j * 256:(j + 1) * 256]
                        mm(SN[0][rows, b * 256:(b + 1) * 256], v0b[:, b, pair, :], pt, **BANK_MM)
                        last = mm(SN[1][rows, b * 256:(b + 1) * 256], ones0_sb, pt, **BANK_MM)
                    last.then_inc(pe_pv, 1)

                scores0(0)
                values1(NC - 1)
                for u in range(1, UNITS0):
                    scores0(u)
                    values0(u - 1)
                if more:
                    project_v1(i + 1)
                values0(UNITS0 - 1)

            def outputs1(j):
                pe.wait_ge(dv_n1, j * 2 + 2)
                if not isinstance(j, int) or j < PAIRS - 1:
                    pe.wait_ge(ac_qk1h, j * 2 + 4)
                    pe.wait_ge(dv_qk1l, j * 2 + 4)
                for n in range(2):
                    last = mm(PR[0][n * S:(n + 1) * S, :], w1o_sb, o1n[:, n].rearrange("p g q -> p (g q)"),
                              **BANK_MM)
                last.then_inc(pe_o1, 1)

            def outputs0(j, half):
                if half == 0:
                    pe.wait_ge(ac_o0h, j + 1)
                    pe.wait_ge(po_o0l, j + 1)
                for r in (2 * half, 2 * half + 1):
                    oh = o0h[:, r].rearrange("p b q -> p (b q)")
                    ol = o0l[:, r].rearrange("p b q -> p (b q)")
                    mm(PR[1][:], oh, woh[:, r, :], start=(r == 0), stop=False)
                    mm(PR[1][:], oh, wol[:, r, :], start=False, stop=False)
                    last = mm(PR[1][:], ol, woh[:, r, :], start=False, stop=(r == REP - 1))
                if half == 1:
                    last.then_inc(pe_o0, 1)

            step(0, True, True)
            pe.wait_ge(set_wo, 2)
            with pe.Fori(1, PAIRS - 1) as i:
                step(i, False, True)
            step(PAIRS - 1, False, False)
            outputs1(PAIRS - 1)
            outputs0(PAIRS - 1, 0)
            outputs0(PAIRS - 1, 1)

        @block.scalar
        def _(act):
            f = nc.scalar.activation

            act.wait_ge(set_pool, 1)
            act.dma_start(low_sb[0:R, :], low).then_inc(set_low, 16)
            act.dma_start(wkv_sb[:], wkv).then_inc(ld_wkv, 16)
            act.dma_start(wq_sb[:], wq).then_inc(ld_wq, 16)
            act.dma_start(v1b[:], ones1).then_inc(ld_v1b, 16)
            act.dma_start(folds_sb[:], folds).then_inc(ld_fold, 16)
            act.dma_start(wo_sb[:], wo).then_inc(ld_wo, 16)

            def high_q1(j):
                after(act, ac_m1, j * 16)
                act.wait_ge(pe_qk1, j * 2 + 1)
                f(q1h[:], PR[0][:], ACT.Identity, bias=b1_sb[:, 0:1]).then_inc(ac_qk1h, 1)

            def high_k1(j):
                act.wait_ge(pe_qk1, j * 2 + 2)
                f(k1h[:], PR[1][:], ACT.Identity, bias=b1_sb[:, 1:2]).then_inc(ac_qk1h, 1)

            def mask_high1(j, group, a, b):
                chunks = slice(group * 4, group * 4 + 4)
                for m in range(a, b):
                    src, dst, sel = ((q1h, qm1h, selq_sb), (k1h, kb1h, selk_sb))[m // 4]
                    act.wait_ge(ac_qk1h, j * 2 + 2)
                    f(dst[:, chunks, m % 4, :],
                      src[:].bitcast(F32).rearrange("p (c q) -> p c q", c=NC)[:, chunks], ACT.Copy,
                      scale=sel[:, m % 4:m % 4 + 1]).then_inc(ac_m1, 1)

            def copy_v1(j):
                act.wait_ge(pe_v1, j + 1)
                for dup in range(2):
                    rows = slice(dup * CH, (dup + 1) * CH)
                    f(v1b[rows, :, :, :, dup * HD1:(dup + 1) * HD1].rearrange("p c n h d -> p c (n h) d"),
                      ST[0][rows].rearrange("p (c m d) -> p c m d", c=NC, d=HD1), ACT.Copy).then_inc(ac_v1, 1)

            act.wait_ge(ld_first, 16 * 2)
            high_q1(0)
            high_k1(0)
            mask_high1(0, 0, 0, 8)
            mask_high1(0, 1, 0, 8)
            act.wait_ge(ld_v1b, 16)
            copy_v1(0)

            def step(i, first, more):
                act.wait_ge(pe_kv0, i + 1)
                f(k0h[:].rearrange("p b t -> p (b t)"), PV[0][:, 0:P], ACT.Copy).then_inc(ac_k0h, 1)
                if first:
                    act.wait_ge(set_pool, 2)
                for dup in range(2):
                    rows = slice(dup * S, (dup + 1) * S)
                    f(v0b[rows, :, :, dup * HD:(dup + 1) * HD],
                      PV[0][rows, P:2 * P].rearrange("p (b m d) -> p b m d", b=2, m=4),
                      ACT.Copy).then_inc(ac_v0, 1)
                act.wait_ge(pe_q0, i + 1)
                f(q0h[:].rearrange("p b r q -> p r b q"),
                  PV[1][:].rearrange("p (r b q) -> p r b q", r=REP, b=2), ACT.Copy).then_inc(ac_q0h, 1)
                if more:
                    high_q1(i + 1)
                mt = ST[1][:].bitcast(BF16)
                act.wait_ge(pe_mt, i * 3 + 2)
                for g in range(2):
                    f(mT1[0:MROWS, g, :], mt[0:MROWS, g * P:(g + 1) * P], ACT.Copy).then_inc(ac_mt, 1)
                if more:
                    high_k1(i + 1)

                def exps(u):
                    act.wait_ge(pe_st, i * UNITS + u + 1)
                    if u < RING:
                        after(act, pe_pv, i * UNITS)
                    else:
                        act.wait_ge(pe_pv, i * UNITS + u - RING + 1)
                    f(pT[:, u % RING, :], ST[u % 2][:], ACT.Exp,
                      scale=SCALE1 if u < UNITS1 else SCALE0).then_inc(ac_ex, 1)

                for u in range(UNITS1):
                    exps(u)
                    if more and u >= 4:
                        mask_high1(i + 1, 0, 2 * (u - 4), 2 * (u - 4) + 2)
                    if u == 2:
                        act.wait_ge(pe_mt, i * 3 + 3)
                        f(mT0[:], SN[0][:].bitcast(BF16)[0:MROWS, 0:P], ACT.Copy).then_inc(ac_mt, 1)
                for u in range(UNITS0):
                    exps(UNITS1 + u)
                    if more and u < UNITS0 - 1:
                        mask_high1(i + 1, 1, 2 * u, 2 * u + 2)
                if more:
                    copy_v1(i + 1)
                    mask_high1(i + 1, 1, 6, 8)
                act.wait_ge(dv_n0, i + 1)
                f(o0h[:].rearrange("p r b q -> p (r b q)"), o0[:].rearrange("p r b q -> p (r b q)"),
                  ACT.Copy).then_inc(ac_o0h, 1)

            step(0, True, True)
            with act.Fori(1, PAIRS - 1) as i:
                step(i, False, True)
            step(PAIRS - 1, False, False)

        @block.gpsimd
        def _(pool):
            g = nc.gpsimd
            g.memset(low_sb[:], 0.0).then_inc(set_pool, 1)
            g.memset(v0b[:], 0.0).then_inc(set_pool, 1)
            g.memset(minus_half[:], -0.5).then_inc(set_pool, 1)

            def set_out(dst, src, sel, blocks, width, done):
                shape = [P, blocks, sel.shape[1], width]
                g.tensor_tensor(dst[:], src.unsqueeze(2).to_broadcast(shape),
                                sel.unsqueeze(1).unsqueeze(3).to_broadcast(shape), ALU.mult).then_inc(done, 1)

            def mask_low1(j):
                pool.wait_ge(dv_qk1l, j * 2 + 2)
                for src, dst, sel in ((q1l, qm1l, selq_sb), (k1l, kb1l, selk_sb)):
                    set_out(dst, src[:].bitcast(F32).rearrange("p (c q) -> p c q", c=NC), sel, NC, CH, po_m1)

            pool.wait_ge(ld_first, 16 * 2)
            mask_low1(0)
            pool.wait_ge(set_pool, 3)

            def low_o0(j):
                pool.wait_ge(ac_o0h, j + 1)
                g.tensor_tensor(o0l[:], o0[:], o0h[:].bitcast(F32), ALU.subtract).then_inc(po_o0l, 1)

            def residual(j):
                pool.wait_ge(ld_xn, j * 16 + 16)
                pool.wait_ge(dv_y, j + 1)
                g.tensor_tensor(y[:], y1[:], xn_sb[:], ALU.add).then_inc(po_y, 1)

            def deviation(j):
                pool.wait_ge(dv_st, j * 2 + 2)
                g.tensor_tensor(rstd[:], vare[:], minus_half[:], ALU.pow).then_inc(po_rstd, 1)

            def step(i, first, more):
                if not first:
                    low_o0(i - 1)
                pool.wait_ge(ac_k0h, i + 1)
                set_out(kb0h, k0h[:].bitcast(F32), sel0_sb, 2, S, po_kb0)
                if not first:
                    residual(i - 1)
                    deviation(i - 1)
                pool.wait_ge(dv_k0l, i + 1)
                set_out(kb0l, k0l[:].bitcast(F32), sel0_sb, 2, S, po_kb0)
                if more:
                    pool.wait_ge(pe_st, i * UNITS + UNITS1)
                    mask_low1(i + 1)

            step(0, True, True)
            with pool.Fori(1, PAIRS - 1) as i:
                step(i, False, True)
            step(PAIRS - 1, False, False)
            low_o0(PAIRS - 1)
            residual(PAIRS - 1)
            deviation(PAIRS - 1)

        @block.vector
        def _(dve):
            v = nc.vector

            dve.wait_ge(ld_mask, 16 * 2)
            for hp in range(2):
                v.tensor_scalar(masked_sb[:, hp], mask_sb[:].rearrange("p (c t) -> p c t", c=NC).unsqueeze(2)
                                .to_broadcast([N, NC, 2, CH]), 0.0, None, ALU.is_le).then_inc(set_mask, 1)

            def low_qk1(j):
                after(dve, po_m1, j * 2)
                for m, (hi, lo) in enumerate(((q1h, q1l), (k1h, k1l))):
                    dve.wait_ge(ac_qk1h, j * 2 + m + 1)
                    v.scalar_tensor_tensor(out=lo[:], in0=PR[m][:], scalar=b1_sb[:, m:m + 1],
                                           in1=hi[:].bitcast(F32), op0=ALU.add,
                                           op1=ALU.subtract).then_inc(dv_qk1l, 1)

            dve.wait_ge(ld_first, 16 * 2)
            low_qk1(0)
            whole = [wkv_sb[:, k, s, :] for k in range(KT) for s in range(2)]
            whole += [wq_sb[:, k].rearrange("p r m -> p (r m)") for k in range(KT)]
            whole += [wo_sb[:, r, :] for r in range(REP)]
            for n, w in enumerate(whole):
                dve.wait_ge(*((ld_wkv, 16) if n < 2 * KT else (ld_wq, 16) if n < 3 * KT else (ld_wo, 16)))
                dve.wait_ge(set_bias, n + 1)
                cols = P if n < 2 * KT else H
                v.scalar_tensor_tensor(out=w, in0=SN[n % 2][:, 0:cols], scalar=LORA, in1=w, op0=ALU.mult,
                                       op1=ALU.add).then_inc(set_w, 1)
            dve.wait_ge(set_bias, LOWS + 1)
            v.tensor_tensor(b1_sb[:, 3:4], PV[0][:, 0:1], b1_sb[:, 2:3], ALU.add).then_inc(set_w, 1)
            flat = "p r n -> p (r n)"
            dve.wait_ge(set_w, LOWS + 1)
            v.tensor_copy(woh[:].rearrange(flat), wo_sb[:].rearrange(flat)).then_inc(set_wo, 1)
            dve.wait_ge(set_wo, 1)
            v.tensor_tensor(wol[:].rearrange(flat), wo_sb[:].rearrange(flat), woh[:].bitcast(F32).rearrange(flat),
                            ALU.subtract).then_inc(set_wo, 1)

            def alone():
                dve.wait_ge(ld_mask, 16)

            def split3(m, p, r, done, at):
                v.tensor_copy(p[0], m).then_inc(done, 1)
                dve.wait_ge(done, at + 1)
                v.tensor_tensor(r[0], m, p[0], ALU.subtract).then_inc(done, 1)
                dve.wait_ge(done, at + 2)
                v.tensor_copy(p[1], r[0]).then_inc(done, 1)
                dve.wait_ge(done, at + 3)
                v.tensor_tensor(r[1], r[0], p[1], ALU.subtract).then_inc(done, 1)
                dve.wait_ge(done, at + 4)
                v.tensor_copy(p[2], r[1]).then_inc(done, 1)

            def masked_y(j):
                dve.wait_ge(pe_o1, j + 1)
                dve.wait_ge(ld_mk, j * 32 + 32)
                v.scalar_tensor_tensor(out=y1[:], in0=PR[0][:], scalar=b1_sb[:, 3:4], in1=mk_sb[:], op0=ALU.add,
                                       op1=ALU.mult).then_inc(dv_y, 1)

            def sum_z(j):
                dve.wait_ge(po_y, j + 1)
                dve.wait_ge(pe_o0, j + 1)
                v.tensor_tensor(z[:], PR[1][:], y[:], ALU.add).then_inc(dv_z, 1)

            def statistics(j):
                dve.wait_ge(dv_z, j + 1)
                v.bn_stats(stats[:], z[:]).then_inc(dv_bn, 1)
                alone()
                dve.wait_ge(dv_bn, j + 1)
                v.bn_aggr(mv[:], stats[:]).then_inc(dv_st, 1)
                dve.wait_ge(dv_st, j * 2 + 1)
                v.tensor_scalar(vare[:], mv[:, 1:2], EPS, None, ALU.add).then_inc(dv_st, 1)

            def normalise(j):
                dve.wait_ge(po_rstd, j + 1)
                after(dve, st_out, j * 16)
                v.tensor_scalar(res[:], z[:], mv[:, 0:1], rstd[:, 0:1], ALU.subtract,
                                ALU.mult).then_inc(dv_out, 1)

            def step(i, first, more):
                for u in range(UNITS1):
                    dve.wait_ge(pe_sn, i * UNITS + u + 1)
                    v.tensor_reduce(m1[:, u // 4, (u % 4) * 8:(u % 4) * 8 + 8],
                                    SN[u % 2][:].rearrange("p (m t) -> p m t", t=CH), AX_X,
                                    ALU.max).then_inc(dv_mx, 1)
                    if u == 2 and not first:
                        masked_y(i - 1)
                    if u == 3:
                        dve.wait_ge(ac_v0, i * 2 + 2)
                        after(dve, po_kb0, i * 2)
                        v.tensor_tensor(k0l[:].rearrange("p b t -> p (b t)"), PV[0][:, 0:P],
                                        k0h[:].bitcast(F32).rearrange("p b t -> p (b t)"),
                                        ALU.subtract).then_inc(dv_k0l, 1)
                    if u == 5 and not first:
                        sum_z(i - 1)
                dve.wait_ge(dv_mx, i * UNITS + UNITS1)
                split3(m1[:], [m1p[:, :, k, :] for k in range(PARTS)], [m1r[:, k] for k in range(2)], dv_p1,
                       i * 5)
                for u in range(UNITS0):
                    dve.wait_ge(pe_sn, i * UNITS + UNITS1 + u + 1)
                    v.tensor_reduce(m0[:, u * NKV:(u + 1) * NKV],
                                    SN[u % 2][:].rearrange("p (m t) -> p m t", t=S), AX_X,
                                    ALU.max).then_inc(dv_mx, 1)
                    if u == 1:
                        dve.wait_ge(ac_q0h, i + 1)
                        v.tensor_tensor(q0l[:].rearrange("p b r q -> p r b q"),
                                        PV[1][:].rearrange("p (r b q) -> p r b q", r=REP, b=2),
                                        q0h[:].bitcast(F32).rearrange("p b r q -> p r b q"),
                                        ALU.subtract).then_inc(dv_q0l, 1)
                dve.wait_ge(dv_mx, i * UNITS + UNITS)
                split3(m0[:], [m0p[:, k, :] for k in range(PARTS)], [m0r[:, k] for k in range(2)], dv_p0,
                       i * 5)
                if not first:
                    statistics(i - 1)
                if more:
                    low_qk1(i + 1)
                if not first:
                    normalise(i - 1)

                for k in range(2):
                    alone()
                    dve.wait_ge(pe_pv, i * UNITS + 4 * k + 4)
                    v.stream_shuffle(sum1[:], PV[k][:], [j % 16 + 16 for j in range(32)]).then_inc(dv_s1, 1)
                    dve.wait_ge(dv_s1, i * 2 + k + 1)
                    v.reciprocal(rec1[:], sum1[:]).then_inc(dv_r1, 1)
                    dve.wait_ge(dv_r1, i * 2 + k + 1)
                    v.tensor_tensor(o1n[:, :, k, :], PV[k][:].rearrange("p (n q) -> p n q", n=2),
                                    rec1[:].rearrange("p (n q) -> p n q", n=2), ALU.mult).then_inc(dv_n1, 1)
                dve.wait_ge(pe_pv, i * UNITS + UNITS)
                v.reciprocal(rec0[:], SN[1][:]).then_inc(dv_r0, 1)
                dve.wait_ge(dv_r0, i + 1)
                after(dve, po_o0l, i)
                v.tensor_tensor(o0[:].rearrange("p r b q -> p b r q"),
                                SN[0][:].rearrange("p (b r q) -> p b r q", b=2, r=REP),
                                rec0[:].rearrange("p (b r q) -> p b r q", b=2, r=REP),
                                ALU.mult).then_inc(dv_n0, 1)

            step(0, True, True)
            with dve.Fori(1, PAIRS - 1) as i:
                step(i, False, True)
            step(PAIRS - 1, False, False)
            masked_y(PAIRS - 1)
            sum_z(PAIRS - 1)
            statistics(PAIRS - 1)
            normalise(PAIRS - 1)


def lay_out(inp):
    import numpy as np

    def bf16(a):
        return (np.asarray(a, np.float32).view(np.uint32) >> 16).astype(np.uint16)

    x, c = np.asarray(inp["x"]), np.asarray(inp["ctx_4096"])

    def turned(a):
        return np.ascontiguousarray(a.reshape(PAIRS, P, KT, P).transpose(0, 3, 2, 1)).reshape(PAIRS * P, KT, P)

    def by_r(a, axis):
        s = a.shape
        a = a.reshape(s[:axis] + (NKV, REP, HD) + s[axis + 1:])
        return np.swapaxes(a, axis, axis + 1).reshape(s)

    def by_half(a):
        return a.reshape(-1, 4, 2, HD).transpose(0, 2, 1, 3).reshape(-1, P)

    g = {k[9:]: np.asarray(v) for k, v in inp.items() if k.startswith("L0_xattn_") or k.startswith("L1_xattn_")}
    out = {
        "xT": turned(x), "xn": x.reshape(N * S, H), "cT": turned(c), "cn": c.reshape(N * S, H),
        "mask": np.asarray(inp["mask_Bx1x4096_ff1"]).reshape(N, H),
        "wq": by_r(g["Wq"], 1).reshape(KT, P, REP, P).transpose(1, 0, 2, 3),
        "wkv": np.stack([g["Wk"], by_half(g["Wv"])], 1).reshape(KT, P, 2, P).transpose(1, 0, 2, 3),
        "wo": by_r(g["Wo"], 0).reshape(REP, P, H).transpose(1, 0, 2),
        "low": np.concatenate([np.stack([g["Ak"].T, g["Av"].T], 1).reshape(R, 2, KT, P).transpose(0, 2, 1, 3)
                               .reshape(R, -1), g["Aq"].T, by_r(g["Ao"], 0).T,
                               g["Bk"], by_half(g["Bv"]), by_r(g["Bq"], 1), g["Bo"]], 1),
    }
    win, bin_, wout, bout = g["W_in"], g["b_in"], g["W_out"], g["b_out"]
    C = 64
    w1 = []
    for k in range(3):
        w = win[k * C:(k + 1) * C]
        both = np.zeros((2, C, 2, C), np.float32)
        for n in range(2):
            both[n, :, n, :] = w.T
        if k == 2:
            both = both.reshape(2, C, 2, 2, 4 * HD1).transpose(0, 1, 3, 2, 4)
        w1.append(both.reshape(P, P))
    out["w1"] = np.stack(w1, 1)
    out["b1v"] = bin_[2 * C:].reshape(C, 1)
    out["w1bias"] = np.concatenate([wout.T, wout.T], 1)
    w1o = np.zeros((4, QD, C), np.float32)
    w1o[:, 0:16] = wout.T.reshape(2, 4, HD1, C).transpose(1, 0, 2, 3).reshape(4, 16, C)
    rows = np.arange(P)
    biases = [np.tile(b, 2).reshape(P, 1) for b in (bin_[0:C], bin_[C:2 * C], bout, np.zeros(C, np.float32))]
    out["consts"] = np.concatenate(biases + [
        (rows[:, None] // HD == np.arange(NKV)).astype(np.float32),
        (rows[:, None] // HD1 % 4 == np.arange(4)).astype(np.float32),
        (rows[:, None] // 32 == np.arange(4)).astype(np.float32),
        np.repeat((rows[:, None] // S == np.arange(2)).astype(np.float32), HD, 1),
        w1o.reshape(P, C)], 1)

    f0 = np.zeros((PARTS, 2, 2, NKV, 2, 2, 4, 2, S), np.float32)
    for b in range(2):
        for rp in range(2):
            for h in range(NKV):
                f0[:, b, rp, h, b, rp, h // 2, h % 2, :] = -1
    folds = np.zeros((P, 18, P), np.float32)
    folds[0:MROWS, 0:16] = f0.reshape(MROWS, 16, P)
    f1 = np.zeros((PARTS, 4, 2, 2, 2, 2, 4, 2, 2, CH), np.float32)
    for c4 in range(4):
        for hp in range(2):
            for n in range(2):
                for half in range(2):
                    f1[:, c4, hp, n, half, hp, c4, n, half, :] = -1
    fold1 = np.zeros((P, 2, 4 * 2 * 2 * CH), np.float32)
    fold1[0:MROWS] = f1.reshape(MROWS, 2, 4 * 2 * 2 * CH)
    out["fold1"] = bf16(fold1)
    neg = np.full(P, -1e9 / SCALE1, np.float32)
    negc = np.zeros((P, P), np.float32)
    for k in range(PARTS):
        negc[MROWS + k] = (neg.view(np.uint32) & 0xFFFF0000).view(np.float32)
        neg = neg - negc[MROWS + k]
    folds[:, 16] = negc
    folds[:, 17] = np.eye(P)
    out["folds"] = bf16(folds)
    o1 = np.zeros((2, CH, NC, 2, 4, 2, 2, HD1), np.float32)
    for half in range(2):
        o1[half, :, :, :, :, 1, half, :] = 1
    out["ones1"] = o1.reshape(P, NC, 2, 4, QD)
    return {k: np.ascontiguousarray(v) for k, v in out.items()}


def kernel(**inputs):
    import concourse.bacc as _bacc
    from concourse.bass_utils import run_bass_kernel_spmd as _run

    nc = _bacc.Bacc("TRN2", target_bir_lowering=False, num_devices=1)
    arrays = lay_out(inputs)
    args = {k: nc.dram_tensor(f"in_{k}", a.shape, mybir.dt.from_np(a.dtype), kind="ExternalInput").ap()
            for k, a in arrays.items()}
    out = nc.dram_tensor("out", (N * S, H), F32, kind="ExternalOutput").ap()
    build(nc, out=out, **args)
    r = _run(nc, [{f"in_{k}": a for k, a in arrays.items()}], core_ids=[0])
    return r.results[0]["out"].reshape(N, S, H)
```

```python
from contextlib import ExitStack

import concourse.bass as bass
from concourse import mybir

F32 = mybir.dt.float32
F32R = mybir.dt.float32r
BF16 = mybir.dt.bfloat16
ACT = mybir.ActivationFunctionType
ALU = mybir.AluOpType
AX_X = mybir.AxisListType.X

N, S, H = 32, 64, 512
PAIRS = N // 2
P = 128
KT = H // P
NKV, REP, HD = 8, 4, 16
R = 16
CH, NC, NH1, HD1 = 64, 8, 8, 8
QD = 32
SCALE0 = HD ** -0.5
SCALE1 = HD1 ** -0.5
LORA = 2.0
EPS = 1e-5
PARTS = 3
MROWS = 32 * PARTS
UNITS1, UNITS0 = NC, 4
UNITS = UNITS1 + UNITS0
RING = 4
LOWS = 16
LOW = LOWS * P + 2 * P + 2 * H
CONSTS = 24 + QD + 2 * S
SROWS = 3 * QD


def low_factors(t, n):
    a = t[:, n * P:(n + 1) * P]
    right = LOWS * P
    if n < 2 * KT:
        return a, t[:, right + (n % 2) * P:right + (n % 2 + 1) * P], P
    right += 2 * P + (0 if n < 3 * KT else H)
    return a, t[:, right:right + H], H


def build(nc, xT, xn, cT, cn, mask, wq, wkv, wo, low, w1, consts, folds, fold1, ones1, b1v, w1bias, out):
    with ExitStack() as ctx:
        def sb(name, shape, dt=F32):
            return ctx.enter_context(nc.sbuf_tensor(name, shape, dt))

        def ps(name, dt=F32):
            return ctx.enter_context(nc.psum_tensor(name, [P, H], dt))

        def sem(name):
            return ctx.enter_context(nc.semaphore(name))

        masked_dram = nc.dram_tensor("masked_rows", (PAIRS, 2 * NC, 2, 2 * CH), BF16, kind="Internal").ap()
        k0_dram = nc.dram_tensor("k0_parts", (2, P, 2 * S), F32, kind="Internal").ap()
        q0_dram = nc.dram_tensor("q0_parts", (2, P, REP * 2 * S), F32, kind="Internal").ap()

        wq_sb = sb("wq_sb", [P, KT, REP, P])
        wkv_sb = sb("wkv_sb", [P, KT, 2, P])
        wo_sb = sb("wo_sb", [P, REP, H])
        woh = sb("woh", [P, REP, H], F32R)
        wol = sb("wol", [P, REP, H], F32R)
        low_sb = sb("low_sb", [P, LOW])
        w1h = sb("w1h", [P, 2, P], F32R)
        w1l = sb("w1l", [P, 2, P], F32R)
        w1_sb = sb("w1_sb", [P, 3, P])
        consts_sb = sb("consts_sb", [P, CONSTS])
        b1v_sb = sb("b1v_sb", [S, 1])
        w1bias_sb = sb("w1bias_sb", [S, P])
        b1_sb = consts_sb[:, 0:4]
        sel0_sb = consts_sb[:, 4:12]
        selq_sb = consts_sb[:, 12:16]
        selk_sb = consts_sb[:, 16:20]
        selh_sb = consts_sb[:, 20:22]
        selg_sb = consts_sb[0:SROWS, 22:24]
        ones0_sb = consts_sb[:, 24:24 + QD]
        selr_sb = consts_sb[:, 22:24]
        w1o_sb = [consts_sb[:, 24 + QD + k * S:24 + QD + (k + 1) * S] for k in range(2)]
        folds_sb = sb("folds_sb", [P, 18, P], BF16)
        fold0_sb = folds_sb[0:MROWS, 0:16, :].rearrange("p (b r m) n -> p b r m n", b=2, r=2)
        negc_sb = folds_sb[:, 16, :]
        ident_sb = folds_sb[:, 17, :]
        fold1_sb = sb("fold1_sb", [P, 2, NC, 2, 2, CH], BF16)

        xT_sb = sb("xT_sb", [P, KT, P])
        cT_sb = sb("cT_sb", [P, KT, P])
        xn_sb = sb("xn_sb", [P, H])
        cn_sb = sb("cn_sb", [P, H])
        mk_sb = sb("mk_sb", [P, H])

        q0h = sb("q0h", [P, 2, REP, S], F32R)
        q0l = sb("q0l", [P, 2, REP, S], F32R)
        k0h = sb("k0h", [P, 2, S], F32R)
        k0l = sb("k0l", [P, 2, S], F32R)
        kb0h = sb("kb0h", [P, 2, NKV, S], F32R)
        qs0 = sb("qs0", [SROWS, 4, 2, REP * S], F32R)
        ks0 = sb("ks0", [SROWS, 4, 2, S])
        kx0 = sb("kx0", [SROWS, 4, 2, 2, S], F32R)
        v0b = sb("v0b", [P, 2, 4, QD])
        m0 = sb("m0", [P, 32])
        m0p = sb("m0p", [P, PARTS, 32], BF16)
        m0r = sb("m0r", [P, 2, 32])
        mT0 = sb("mT0", [MROWS, P], BF16)
        w0 = sb("w0", [P, 2, REP * S])
        rec0 = sb("rec0", [P, 2, REP * S])
        o0 = sb("o0", [P, REP, 2, S])
        o0h = sb("o0h", [P, REP, 2, S], F32R)
        o0l = sb("o0l", [P, REP, 2, S], F32R)

        cnh = sb("cnh", [P, H], F32R)
        cnl = sb("cnl", [P, H], F32R)
        q1h = sb("q1h", [P, H], F32R)
        q1l = sb("q1l", [P, H], F32R)
        k1h = sb("k1h", [P, H], F32R)
        k1l = sb("k1l", [P, H], F32R)
        qm1h = sb("qm1h", [P, NC, 4, CH], F32R)
        kb1h = sb("kb1h", [P, NC, 4, CH], F32R)
        qs1 = sb("qs1", [P, 2, H])
        ks1 = sb("ks1", [P, 2, H])
        qx1 = sb("qx1", [P, NC, 2, 4, CH], F32R)
        kx1 = sb("kx1", [P, NC, 4, CH], F32R)
        v1b = sb("v1b", [P, NC, 2, 4, QD])
        m1 = sb("m1", [P, 2, 32])
        m1p = sb("m1p", [P, 2, PARTS, 32], BF16)
        m1r = sb("m1r", [P, 2, 2, 32])
        mT1 = sb("mT1", [P, 2, P], BF16)
        odd1 = sb("odd1", [P, 2, 2, 2, CH])
        sum1 = sb("sum1", [P, 2, 4 * CH])
        rec1 = sb("rec1", [P, 2, 4 * CH])
        o1n = sb("o1n", [P, 2, 2, 2, 2, CH])

        pT = sb("pT", [P, RING, H])
        mask_sb = pT[0:N, 0, :]
        masked_sb = pT[0:N, 1:3, :].rearrange("p a b -> p (a b)").bitcast(BF16).rearrange(
            "p (a c h t) -> p a c h t", a=2, c=NC, h=2)

        y1 = sb("y1", [P, H])
        y = sb("y", [P, H])
        z = sb("z", [P, H])
        stats = sb("stats", [P, 6])
        mv = sb("mv", [P, 2])
        vare = sb("vare", [P, 1])
        minus_half = sb("minus_half", [P, 1])
        rstd = sb("rstd", [P, 1])
        res = sb("res", [P, H])

        SN = [ps("sn0"), ps("sn1")]
        ST = [ps("st0"), ps("st1")]
        PR = [ps("pr0"), ps("pr1")]
        PV = [ps("pv0"), ps("pv1")]

        ld_first = sem("ld_first")
        ld_wkv = sem("ld_wkv")
        ld_wq = sem("ld_wq")
        ld_wo = sem("ld_wo")
        ld_mask = sem("ld_mask")
        ld_fold = sem("ld_fold")
        ld_v1b = sem("ld_v1b")
        ld_bias = sem("ld_bias")
        ld_x = sem("ld_x")
        ld_c = sem("ld_c")
        ld_cn = sem("ld_cn")
        ld_xn = sem("ld_xn")
        ld_mk = sem("ld_mk")
        ld_km = sem("ld_km")
        ld_k0 = sem("ld_k0")
        ld_q0 = sem("ld_q0")
        ld_q1 = sem("ld_q1")
        ld_k1 = sem("ld_k1")
        st_km = sem("st_km")
        st_k0 = sem("st_k0")
        st_q0 = sem("st_q0")
        st_out = sem("st_out")
        set_mask = sem("set_mask")
        set_w = sem("set_w")
        set_bias = sem("set_bias")
        set_wo = sem("set_wo")
        set_pool = sem("set_pool")
        set_clear = sem("set_clear")
        set_low = sem("set_low")
        pe_kv0 = sem("pe_kv0")
        pe_q0 = sem("pe_q0")
        pe_sn = sem("pe_sn")
        pe_qk1 = sem("pe_qk1")
        pe_v1 = sem("pe_v1")
        pe_mt = sem("pe_mt")
        pe_st = sem("pe_st")
        pe_pv = sem("pe_pv")
        pe_o1 = sem("pe_o1")
        pe_o0 = sem("pe_o0")
        ac_q0h = sem("ac_q0h")
        ac_k0h = sem("ac_k0h")
        ac_v0 = sem("ac_v0")
        set_w1 = sem("set_w1")
        ac_cnh = sem("ac_cnh")
        dv_cnl = sem("dv_cnl")
        ac_qk1h = sem("ac_qk1h")
        ac_mt = sem("ac_mt")
        ac_ex = sem("ac_ex")
        ac_v1 = sem("ac_v1")
        ac_m1 = sem("ac_m1")
        ac_odd1 = sem("ac_odd1")
        ac_w0 = sem("ac_w0")
        ac_o0h = sem("ac_o0h")
        dv_q0l = sem("dv_q0l")
        dv_k0l = sem("dv_k0l")
        dv_mx = sem("dv_mx")
        dv_p1 = sem("dv_p1")
        dv_p0 = sem("dv_p0")
        dv_qk1l = sem("dv_qk1l")
        dv_s1 = sem("dv_s1")
        dv_r1 = sem("dv_r1")
        dv_n1 = sem("dv_n1")
        dv_r0 = sem("dv_r0")
        dv_n0 = sem("dv_n0")
        dv_y = sem("dv_y")
        dv_z = sem("dv_z")
        dv_bn = sem("dv_bn")
        dv_st = sem("dv_st")
        dv_out = sem("dv_out")
        po_kb0 = sem("po_kb0")
        po_m1 = sem("po_m1")
        po_y = sem("po_y")
        po_o0l = sem("po_o0l")
        po_rstd = sem("po_rstd")

        fold1, folds = (a.bitcast(BF16) for a in (fold1, folds))
        BANK_MM = dict(start=True, stop=True)
        block = ctx.enter_context(nc.Block())

        def after(eng, signal, count):
            if not isinstance(count, int) or count > 0:
                eng.wait_ge(signal, count)

        @block.sync
        def _(sp):
            def load_x(j):
                sp.dma_start(xT_sb[:], xT[bass.ds(j * P, P)]).then_inc(ld_x, 16)

            def load_c(j):
                sp.dma_start(cT_sb[:], cT[bass.ds(j * P, P)]).then_inc(ld_c, 16)

            def load_cn(j):
                sp.dma_start(cn_sb[:], cn[bass.ds(j * P, P), :]).then_inc(ld_cn, 16)

            def load_rows(j):
                sp.dma_start(xn_sb[:], xn[bass.ds(j * P, P), :]).then_inc(ld_xn, 16)
                for n in range(2):
                    sp.dma_start(mk_sb[n * S:(n + 1) * S, :],
                                 mask[bass.ds(j * 2 + n, 1), :].to_broadcast([S, H])).then_inc(ld_mk, 16)

            def part_out(dram, m, part, ready, j, stored):
                sp.wait_ge(ready, j + 1)
                sp.dma_start(dram[m], part).then_inc(stored, 16)

            def stack(dst, dram, order, stored, j, done):
                sp.wait_ge(stored, j * 32 + 32)
                for k, m in enumerate(order):
                    sp.dma_start(dst[k * QD:(k + 1) * QD],
                                 dram[m].rearrange("(a p) n -> p a n", a=4)).then_inc(done, 16)

            def spread_qk1(j, m, high):
                part, dst, done = ((q1l, q1h)[high], qs1, ld_q1) if m == 0 else ((k1l, k1h)[high], ks1, ld_k1)
                if m == 0 and high:
                    after(sp, po_m1, j * 8)
                sp.wait_ge(ac_qk1h if high else dv_qk1l, j * 2 + m + 1)
                for n in range(2):
                    to = n if high == (m == 0) else 1 - n
                    sp.dma_start(dst[to * S:(to + 1) * S, n, :],
                                 part[n * S:(n + 1) * S, :].bitcast(F32)).then_inc(done, 16)

            def load_masked(j):
                sp.dma_start(fold1_sb[MROWS:MROWS + PARTS].rearrange("p a c n h t -> p (a c n h t)"),
                             masked_dram[bass.ds(j, 1)].rearrange("o a n k -> o (a n k)")
                             .to_broadcast([PARTS, 4 * NC * 2 * CH])).then_inc(ld_km, 16)

            load_cn(0)
            sp.dma_start(w1_sb[:], w1).then_inc(ld_first, 16)
            sp.dma_start(consts_sb[:], consts).then_inc(ld_first, 16)
            sp.wait_ge(set_pool, 1)
            sp.wait_ge(set_clear, 1)
            sp.dma_start(low_sb[0:R, :], low).then_inc(set_low, 16)
            sp.dma_start(wkv_sb[:], wkv).then_inc(ld_wkv, 16)
            for n in range(2):
                sp.dma_start(mask_sb[n * PAIRS:(n + 1) * PAIRS],
                             mask.rearrange("(j n) h -> n j h", n=2)[n]).then_inc(ld_mask, 16)
            sp.dma_start(wq_sb[:], wq).then_inc(ld_wq, 16)
            sp.dma_start(v1b[:], ones1).then_inc(ld_v1b, 16)
            sp.dma_start(w1bias_sb[:], w1bias).then_inc(ld_bias, 16)
            sp.dma_start(b1v_sb[:], b1v).then_inc(ld_bias, 16)
            sp.wait_ge(set_mask, 2)
            for n in range(2):
                sp.dma_start(masked_dram[:, :, n, :], masked_sb[n * PAIRS:(n + 1) * PAIRS]
                             .rearrange("p a c h t -> p (a c) (h t)")).then_inc(st_km, 16)
            load_c(0)
            for hp in range(2):
                for g in range(2):
                    sp.dma_start(fold1_sb[:, hp, g * 4:(g + 1) * 4].rearrange("p c n h t -> p (c n h t)"),
                                 fold1[:, hp]).then_inc(ld_fold, 16)
            sp.dma_start(folds_sb[:], folds).then_inc(ld_fold, 16)
            for g in range(2):
                sp.dma_start(mT1[:, g, :], folds[:, 16, :]).then_inc(ld_fold, 16)
            sp.wait_ge(st_km, 16 * 2)
            sp.wait_ge(ld_fold, 16 * 7)
            load_masked(0)
            load_x(0)
            sp.dma_start(wo_sb[:], wo).then_inc(ld_wo, 16)
            for m in range(2):
                for high in (True, False):
                    spread_qk1(0, m, high)
            sp.wait_ge(pe_v1, 1)
            load_cn(1)
            load_rows(0)

            def step(i, more, more_cn):
                if more:
                    sp.wait_ge(pe_kv0, i + 1)
                    load_c(i + 1)
                after(sp, ld_k0, i * 48)
                part_out(k0_dram, 0, k0h[:].bitcast(F32).rearrange("p b t -> p (b t)"), ac_k0h, i, st_k0)
                part_out(k0_dram, 1, k0l[:].bitcast(F32).rearrange("p b t -> p (b t)"), dv_k0l, i, st_k0)
                after(sp, po_kb0, i * 2)
                stack(ks0[:].rearrange("p a b t -> p a (b t)"), k0_dram, (0, 0, 1), st_k0, i, ld_k0)
                after(sp, ld_q0, i * 48)
                part_out(q0_dram, 0, q0h[:].bitcast(F32).rearrange("p b r q -> p (b r q)"), ac_q0h, i, st_q0)
                part_out(q0_dram, 1, q0l[:].bitcast(F32).rearrange("p b r q -> p (b r q)"), dv_q0l, i, st_q0)
                if more:
                    sp.wait_ge(pe_q0, i + 1)
                    load_x(i + 1)
                    spread_qk1(i + 1, 0, True)
                    spread_qk1(i + 1, 1, True)
                stack(qs0[:].bitcast(F32).rearrange("p a b m -> p a (b m)"), q0_dram, (0, 1, 0), st_q0, i, ld_q0)
                if more:
                    spread_qk1(i + 1, 0, False)
                    spread_qk1(i + 1, 1, False)
                after(sp, dv_out, i)
                if not isinstance(i, int) or i > 0:
                    sp.dma_start(out[bass.ds((i - 1) * P, P), :], res[:]).then_inc(st_out, 16)
                    load_rows(i)
                if more:
                    sp.wait_ge(pe_st, i * UNITS + UNITS1)
                    load_masked(i + 1)
                if more_cn:
                    sp.wait_ge(pe_v1, i + 2)
                    load_cn(i + 2)

            step(0, True, True)
            with sp.Fori(1, PAIRS - 2) as i:
                step(i, True, True)
            step(PAIRS - 2, True, False)
            step(PAIRS - 1, False, False)
            sp.wait_ge(dv_out, PAIRS)
            sp.dma_start(out[(PAIRS - 1) * P:PAIRS * P, :], res[:]).then_inc(st_out, 16)
            sp.wait_ge(st_out, 16 * PAIRS)

        @block.tensor
        def _(pe):
            mm = nc.tensor.matmul

            def project_qk1(m):
                mm(PR[m][:], w1h[:, m], cnh[:], start=True, stop=False)
                mm(PR[m][:], w1l[:, m], cnh[:], start=False, stop=False)
                mm(PR[m][:], w1h[:, m], cnl[:], start=False, stop=True).then_inc(pe_qk1, 1)

            def project_v1(j, a, b):
                if a == 0:
                    after(pe, ac_ex, j * UNITS - 1)
                for c in range(a, b):
                    last = mm(ST[0][:, c * P:(c + 1) * P], cn_sb[:, c * P:(c + 1) * P], w1_sb[:, 2, :], **BANK_MM)
                if b == NC // 2:
                    last.then_inc(pe_v1, 1)

            pe.wait_ge(ld_first, 16 * 2)
            pe.wait_ge(ld_cn, 16)
            for m in range(2):
                mm(PR[m][:], w1_sb[:, m], cn_sb[:], **BANK_MM).then_inc(pe_qk1, 1)
            project_v1(0, 0, NC // 2)

            def low_product(n, bank):
                a, b, w = low_factors(low_sb, n)
                mm(bank[:, 0:w], a, b, **BANK_MM).then_inc(set_bias, 1)

            pe.wait_ge(set_low, 16)
            for n in range(3 * KT):
                if n >= 2:
                    pe.wait_ge(set_w, n - 1)
                low_product(n, SN[n % 2])
            pe.wait_ge(set_w, 3 * KT - 1)
            pe.wait_ge(ld_bias, 16 * 2)
            mm(SN[0][:, 0:1], w1bias_sb[:], b1v_sb[:], **BANK_MM).then_inc(set_bias, 1)
            pe.wait_ge(set_w, 2 * KT)
            pe.wait_ge(ld_fold, 16 * 7)

            def step(i, first, more):
                def maxima1(c):
                    if c == 0:
                        after(pe, dv_n0, i * 2 - 1)
                    elif c == 1:
                        after(pe, ac_w0, i)
                    else:
                        pe.wait_ge(dv_mx, i * UNITS + c - 1)
                    for hp in range(2):
                        o = SN[c % 2][:, hp * 256:(hp + 1) * 256]
                        mm(o, qm1h[:, c, 2 * hp:2 * hp + 2, :].rearrange("p h q -> p (h q)"),
                           kb1h[:, c].rearrange("p a t -> p (a t)"), start=(hp == 0), stop=False)
                    for hp in range(2):
                        last = mm(SN[c % 2][:, hp * 256:(hp + 1) * 256], negc_sb,
                                  fold1_sb[:, 0, c].rearrange("p n h t -> p (n h t)"), start=False, stop=(hp == 1))
                    last.then_inc(pe_sn, 1)

                def maxima0(u):
                    b, rp = u // 2, u % 2
                    pe.wait_ge(dv_mx, i * UNITS + UNITS1 + u - 1)
                    mm(SN[u % 2][:], q0h[:, b, 2 * rp:2 * rp + 2, :].rearrange("p r q -> p (r q)"),
                       kb0h[:, b].rearrange("p g t -> p (g t)"), **BANK_MM).then_inc(pe_sn, 1)

                def project_q0(r):
                    for k in range(KT):
                        last = mm(PV[1][:, r * P:(r + 1) * P], wq_sb[:, k, r, :], xT_sb[:, k, :],
                                  start=(k == 0), stop=(k == KT - 1))
                    if r == REP - 1:
                        last.then_inc(pe_q0, 1)

                pe.wait_ge(ld_c, i * 16 + 16)
                after(pe, dv_n1, i * 4 - 2)
                for k in range(KT):
                    mm(PV[0][:, 0:P], wkv_sb[:, k, 0, :], cT_sb[:, k, :], start=(k == 0), stop=(k == KT - 1))
                for k in range(KT):
                    last = mm(PV[0][:, P:2 * P], cT_sb[:, k, :], wkv_sb[:, k, 1, :], start=(k == 0),
                              stop=(k == KT - 1))
                last.then_inc(pe_kv0, 1)
                if first:
                    pe.wait_ge(set_w, 3 * KT + 1)
                pe.wait_ge(ac_m1, i * 16 + 8)
                pe.wait_ge(ld_km, i * 16 + 16)
                maxima1(0)
                if not first:
                    outputs1(i - 1)
                else:
                    pe.wait_ge(dv_qk1l, 2)
                    for n in range(2):
                        low_product(3 * KT + n, PR[n])
                maxima1(1)
                pe.wait_ge(ld_x, i * 16 + 16)
                after(pe, dv_n1, i * 4)
                project_q0(0)
                maxima1(2)
                project_q0(1)
                maxima1(3)
                project_q0(2)
                pe.wait_ge(ac_m1, i * 16 + 16)
                maxima1(4)
                if first:
                    for n in range(2, 4):
                        pe.wait_ge(set_w, 3 * KT + n)
                        low_product(3 * KT + n, PR[n % 2])
                maxima1(5)
                project_q0(3)
                maxima1(6)
                maxima1(7)
                if not first:
                    outputs0(i - 1, 0)
                if first:
                    pe.wait_ge(set_w, LOWS + 1)
                if more:
                    after(pe, dv_y, i)
                    if first:
                        pe.wait_ge(set_w1, 2)
                    pe.wait_ge(ac_cnh, i + 1)
                    pe.wait_ge(dv_cnl, i + 1)
                    project_qk1(0)
                pe.wait_ge(po_kb0, i * 2 + 1)
                pe.wait_ge(ac_q0h, i + 1)
                maxima0(0)
                maxima0(1)

                pe.wait_ge(dv_p1, i * 5 + 5)
                mt = ST[1][:].bitcast(BF16)
                for g in range(2):
                    nc.tensor.transpose(mt[0:MROWS, g * P:(g + 1) * P], m1p[:, g].rearrange("p a m -> p (a m)"),
                                        ident_sb).then_inc(pe_mt, 1)
                if not first:
                    outputs0(i - 1, 1)

                def scores1(c):
                    if c == 0:
                        pe.wait_ge(po_m1, i * 8 + 4)
                        pe.wait_ge(ac_mt, i * 3 + 2)
                        pe.wait_ge(ac_v1, i * 4 + 4)
                    elif c > 1:
                        pe.wait_ge(ac_ex, i * UNITS + c - 1)
                    if c == 4:
                        pe.wait_ge(po_m1, i * 8 + 8)
                    for n in range(2):
                        o = ST[c % 2][:, n * 256:(n + 1) * 256]
                        kh = kb1h[:, c, 2 * n:2 * n + 2, :].rearrange("p h t -> p (h t)")
                        kx = kx1[:, c, 2 * n:2 * n + 2, :].rearrange("p h t -> p (h t)")
                        mm(o, kh, qm1h[:, c].rearrange("p h q -> p (h q)"), start=(n == 0), stop=False)
                        mm(o, kx, qx1[:, c, n].rearrange("p h q -> p (h q)"), start=False, stop=False)
                    for n in range(2):
                        o = ST[c % 2][:, n * 256:(n + 1) * 256]
                        for hp in range(2):
                            last = mm(o[:, hp * P:(hp + 1) * P],
                                      fold1_sb[:, hp, c, n].rearrange("p h t -> p (h t)"),
                                      mT1[:, c // 4, :], start=False, stop=(n == 1 and hp == 1))
                    last.then_inc(pe_st, 1)

                def values1(c):
                    if c == 0:
                        pe.wait_ge(ac_v0, i * 4 + 4)
                        pe.wait_ge(dv_k0l, i + 1)
                        pe.wait_ge(dv_q0l, i + 1)
                    pe.wait_ge(ac_ex, i * UNITS + c + 1)
                    for n in range(2):
                        for h in range(4):
                            last = mm(PV[c // 4][h * QD:(h + 1) * QD,
                                                 (n * 4 + c % 4) * CH:(n * 4 + c % 4 + 1) * CH],
                                      v1b[:, c, n, h, :],
                                      pT[:, c % RING, (n * 4 + h) * CH:(n * 4 + h + 1) * CH], **BANK_MM)
                    last.then_inc(pe_pv, 1)

                for c in range(NC):
                    scores1(c)
                    if c < 2:
                        maxima0(2 + c)
                    if c == 1 and more:
                        after(pe, dv_z, i)
                        project_qk1(1)
                    if c >= 1:
                        values1(c - 1)
                    if c == 4:
                        pe.wait_ge(dv_p0, i * 5 + 5)
                        nc.tensor.transpose(SN[0][:].bitcast(BF16)[0:MROWS, 0:P],
                                            m0p[:].rearrange("p a m -> p (a m)"), ident_sb).then_inc(pe_mt, 1)

                def scores0(u):
                    if u == 0:
                        pe.wait_ge(ac_mt, i * 3 + 3)
                        pe.wait_ge(po_kb0, i * 2 + 2)
                        pe.wait_ge(ld_q0, i * 48 + 48)
                    pe.wait_ge(ac_ex, i * UNITS + UNITS1 + u - 1)
                    b = u // 2
                    for j in range(2):
                        pair = 2 * (u % 2) + j
                        o = ST[u % 2][:, j * 256:(j + 1) * 256]
                        mm(o, kx0[:, pair, b].rearrange("p g t -> p (g t)"), qs0[:, pair, b], start=(j == 0),
                           stop=False)
                    for j in range(2):
                        pair = 2 * (u % 2) + j
                        o = ST[u % 2][:, j * 256:(j + 1) * 256]
                        for rp in range(2):
                            last = mm(o[:, rp * P:(rp + 1) * P], fold0_sb[:, b, rp, pair, :], mT0[:],
                                      start=False, stop=(j == 1 and rp == 1))
                    last.then_inc(pe_st, 1)

                def values0(u):
                    pe.wait_ge(ac_ex, i * UNITS + UNITS1 + u + 1)
                    b = u // 2
                    for j in range(2):
                        pair = 2 * (u % 2) + j
                        rows = slice(pair * QD, (pair + 1) * QD)
                        pt = pT[:, u % RING, j * 256:(j + 1) * 256]
                        mm(SN[b][rows, 0:256], v0b[:, b, pair, :], pt, **BANK_MM)
                        last = mm(SN[b][rows, 256:512], ones0_sb, pt, **BANK_MM)
                    last.then_inc(pe_pv, 1)

                scores0(0)
                values1(NC - 1)
                for u in range(1, UNITS0):
                    scores0(u)
                    values0(u - 1)
                if more:
                    project_v1(i + 1, 0, NC // 4)
                values0(UNITS0 - 1)
                if more:
                    project_v1(i + 1, NC // 4, NC // 2)

            def outputs1(j):
                pe.wait_ge(dv_n1, j * 4 + 4)
                if not isinstance(j, int) or j < PAIRS - 1:
                    pe.wait_ge(ac_qk1h, j * 2 + 4)
                    pe.wait_ge(dv_qk1l, j * 2 + 4)
                for n in range(2):
                    for odd in range(2):
                        last = mm(PR[0][n * S:(n + 1) * S].rearrange("p (g c o q) -> p o g c q", g=2, c=2, q=CH)[:, odd],
                                  w1o_sb[odd], o1n[:, :, odd, n], **BANK_MM)
                last.then_inc(pe_o1, 1)

            def outputs0(j, half):
                if half == 0:
                    pe.wait_ge(ac_o0h, j + 1)
                    pe.wait_ge(po_o0l, j + 1)
                for r in (2 * half, 2 * half + 1):
                    oh = o0h[:, r].rearrange("p b q -> p (b q)")
                    ol = o0l[:, r].rearrange("p b q -> p (b q)")
                    mm(PR[1][:], oh, woh[:, r, :], start=(r == 0), stop=False)
                    mm(PR[1][:], oh, wol[:, r, :], start=False, stop=False)
                    last = mm(PR[1][:], ol, woh[:, r, :], start=False, stop=(r == REP - 1))
                if half == 1:
                    last.then_inc(pe_o0, 1)

            step(0, True, True)
            pe.wait_ge(set_wo, 2)
            with pe.Fori(1, PAIRS - 1) as i:
                step(i, False, True)
            step(PAIRS - 1, False, False)
            outputs1(PAIRS - 1)
            pe.wait_ge(dv_n0, 2 * PAIRS)
            for k in range(REP):
                last = mm(PR[1][:], o0[:, k].rearrange("p b q -> p (b q)"), wo_sb[:, k, :], start=(k == 0),
                          stop=(k == REP - 1))
            last.then_inc(pe_o0, 1)

        @block.scalar
        def _(act):
            f = nc.scalar.activation

            def high_q1(j):
                after(act, ac_m1, j * 16)
                after(act, ld_q1, j * 64)
                after(act, ld_k1, j * 64)
                act.wait_ge(pe_qk1, j * 2 + 1)
                f(q1h[:], PR[0][:], ACT.Identity, bias=b1_sb[:, 0:1]).then_inc(ac_qk1h, 1)

            def high_k1(j):
                act.wait_ge(pe_qk1, j * 2 + 2)
                f(k1h[:], PR[1][:], ACT.Identity, bias=b1_sb[:, 1:2]).then_inc(ac_qk1h, 1)

            def mask_high1(j, group, a, b):
                chunks = slice(group * 4, group * 4 + 4)
                for m in range(a, b):
                    src, dst, sel = ((q1h, qm1h, selq_sb), (k1h, kb1h, selk_sb))[m // 4]
                    act.wait_ge(ac_qk1h, j * 2 + 2)
                    f(dst[:, chunks, m % 4, :],
                      src[:].bitcast(F32).rearrange("p (c q) -> p c q", c=NC)[:, chunks], ACT.Copy,
                      scale=sel[:, m % 4:m % 4 + 1]).then_inc(ac_m1, 1)

            def copy_v1(j):
                act.wait_ge(pe_v1, j + 1)
                for dup in range(2):
                    for odd in range(2):
                        f(v1b[dup * CH:(dup + 1) * CH, odd::2, :, :, (2 * odd + dup) * HD1:(2 * odd + dup + 1) * HD1]
                          .rearrange("p c n h d -> p c (n h) d"),
                          ST[0][odd * CH:(odd + 1) * CH].rearrange("p (c s m d) -> p c s m d", c=NC // 2, s=2,
                                                                   d=HD1)[:, :, dup], ACT.Copy).then_inc(ac_v1, 1)

            def high_o0(j):
                act.wait_ge(dv_n0, j * 2 + 2)
                f(o0h[:].rearrange("p r b q -> p (r b q)"), o0[:].rearrange("p r b q -> p (r b q)"),
                  ACT.Copy).then_inc(ac_o0h, 1)

            act.wait_ge(ld_first, 16 * 2)
            high_q1(0)
            high_k1(0)
            f(w1h[:], w1_sb[:, 0:2], ACT.Copy).then_inc(set_w1, 1)
            mask_high1(0, 0, 0, 8)
            mask_high1(0, 1, 0, 8)
            act.wait_ge(ld_v1b, 16)
            copy_v1(0)

            def step(i, first, more):
                if more:
                    act.wait_ge(ld_cn, i * 16 + 32)
                    f(cnh[:], cn_sb[:], ACT.Copy).then_inc(ac_cnh, 1)
                act.wait_ge(pe_kv0, i + 1)
                after(act, ld_k0, i * 48)
                f(k0h[:].rearrange("p b t -> p (b t)"), PV[0][:, 0:P], ACT.Copy).then_inc(ac_k0h, 1)
                if first:
                    act.wait_ge(set_pool, 2)
                for dup in range(2):
                    for b in range(2):
                        f(v0b[dup * S:(dup + 1) * S, b, :, dup * HD:(dup + 1) * HD],
                          PV[0][b * S:(b + 1) * S, P + dup * S:P + (dup + 1) * S]
                          .rearrange("p (m d) -> p m d", m=4), ACT.Copy).then_inc(ac_v0, 1)
                if not first:
                    high_o0(i - 1)
                act.wait_ge(pe_q0, i + 1)
                after(act, ld_q0, i * 48)
                f(q0h[:].rearrange("p b r q -> p r b q"),
                  PV[1][:].rearrange("p (r b q) -> p r b q", r=REP, b=2), ACT.Copy).then_inc(ac_q0h, 1)
                if more:
                    high_q1(i + 1)
                mt = ST[1][:].bitcast(BF16)
                act.wait_ge(pe_mt, i * 3 + 2)
                for g in range(2):
                    f(mT1[0:MROWS, g, :], mt[0:MROWS, g * P:(g + 1) * P], ACT.Copy).then_inc(ac_mt, 1)

                def exps(u):
                    act.wait_ge(pe_st, i * UNITS + u + 1)
                    if u < RING:
                        after(act, pe_pv, i * UNITS)
                    else:
                        act.wait_ge(pe_pv, i * UNITS + u - RING + 1)
                    f(pT[:, u % RING, :], ST[u % 2][:], ACT.Exp,
                      scale=SCALE1 if u < UNITS1 else SCALE0).then_inc(ac_ex, 1)

                def odd_sums(k):
                    act.wait_ge(pe_pv, i * UNITS + 4 * k + 4)
                    after(act, dv_s1, i * 4 - 2 * (1 - k))
                    f(odd1[:, k], PV[k][:].rearrange("p (n c o q) -> p o n c q", n=2, o=2, q=CH)[:, 1], ACT.Copy,
                      scale=selr_sb[:, 0:1]).then_inc(ac_odd1, 1)

                for u in range(UNITS1):
                    exps(u)
                    if u == 4:
                        odd_sums(0)
                    if more and u == 1:
                        high_k1(i + 1)
                    if more and u >= 3:
                        mask_high1(i + 1, 0, u - 3, u - 2)
                    if u == 4:
                        act.wait_ge(pe_mt, i * 3 + 3)
                        f(mT0[:], SN[0][:].bitcast(BF16)[0:MROWS, 0:P], ACT.Copy).then_inc(ac_mt, 1)
                for u in range(UNITS0):
                    exps(UNITS1 + u)
                    if u == 0:
                        odd_sums(1)
                    elif more and u < UNITS0 - 1:
                        mask_high1(i + 1, 0, u + 4, u + 5)
                act.wait_ge(pe_pv, i * UNITS + UNITS)
                after(act, dv_n0, i * 2)
                f(w0[:].rearrange("p s m -> p (s m)"), SN[1][:], ACT.Copy).then_inc(ac_w0, 1)
                if more:
                    mask_high1(i + 1, 0, 7, 8)
                    copy_v1(i + 1)
                if more:
                    mask_high1(i + 1, 1, 0, 8)

            step(0, True, True)
            with act.Fori(1, PAIRS - 1) as i:
                step(i, False, True)
            step(PAIRS - 1, False, False)

        @block.gpsimd
        def _(pool):
            g = nc.gpsimd
            g.memset(low_sb[:, 0:LOW // 2], 0.0).then_inc(set_pool, 1)
            g.memset(v0b[:], 0.0).then_inc(set_pool, 1)
            g.memset(minus_half[:], -0.5).then_inc(set_pool, 1)

            def set_out(dst, src, sel, blocks, width, done):
                shape = [src.shape[0], blocks, sel.shape[1], width]
                g.tensor_tensor(dst, src.unsqueeze(2).to_broadcast(shape),
                                sel.unsqueeze(1).unsqueeze(3).to_broadcast(shape), ALU.mult).then_inc(done, 1)

            def set_low1(j, group):
                chunks = slice(group * 4, group * 4 + 4)
                pool.wait_ge(ld_q1, j * 64 + 64)
                for n in range(2):
                    set_out(qx1[:, chunks, n], qs1[:, n].rearrange("p (c q) -> p c q", c=NC)[:, chunks], selq_sb,
                            4, CH, po_m1)
                pool.wait_ge(ld_k1, j * 64 + 64)
                for n in range(2):
                    set_out(kx1[:, chunks, 2 * n:2 * n + 2],
                            ks1[:, n].rearrange("p (c t) -> p c t", c=NC)[:, chunks], selh_sb, 4, CH, po_m1)

            pool.wait_ge(ld_first, 16 * 2)
            pool.wait_ge(set_pool, 3)

            def low_o0(j):
                pool.wait_ge(ac_o0h, j + 1)
                g.tensor_tensor(o0l[:], o0[:], o0h[:].bitcast(F32), ALU.subtract).then_inc(po_o0l, 1)

            def residual(j):
                pool.wait_ge(ld_xn, j * 16 + 16)
                pool.wait_ge(dv_y, j + 1)
                g.tensor_tensor(y[:], y1[:], xn_sb[:], ALU.add).then_inc(po_y, 1)

            def deviation(j):
                pool.wait_ge(dv_st, j * 2 + 2)
                g.tensor_tensor(rstd[:], vare[:], minus_half[:], ALU.pow).then_inc(po_rstd, 1)

            def step(i, first, more):
                if not first:
                    low_o0(i - 1)
                pool.wait_ge(ac_k0h, i + 1)
                set_out(kb0h[:], k0h[:].bitcast(F32), sel0_sb, 2, S, po_kb0)
                if first:
                    set_low1(0, 0)
                    set_low1(0, 1)
                if not first:
                    residual(i - 1)
                pool.wait_ge(ld_k0, i * 48 + 48)
                set_out(kx0[:].rearrange("p a b g t -> p (a b) g t"), ks0[:].rearrange("p a b t -> p (a b) t"),
                        selg_sb, 8, S, po_kb0)
                if not first:
                    deviation(i - 1)
                if more:
                    for group in range(2):
                        pool.wait_ge(pe_st, i * UNITS + 4 * group + 4)
                        set_low1(i + 1, group)

            step(0, True, True)
            with pool.Fori(1, PAIRS - 1) as i:
                step(i, False, True)
            step(PAIRS - 1, False, False)
            residual(PAIRS - 1)
            deviation(PAIRS - 1)

        @block.vector
        def _(dve):
            v = nc.vector

            v.memset(low_sb[:, LOW // 2:], 0.0).then_inc(set_clear, 1)
            dve.wait_ge(ld_mask, 16 * 2)
            for hp in range(2):
                v.tensor_scalar(masked_sb[:, hp], mask_sb.rearrange("p (c t) -> p c t", c=NC).unsqueeze(2)
                                .to_broadcast([N, NC, 2, CH]), 0.0, None, ALU.is_le).then_inc(set_mask, 1)

            def low_qk1(j):
                after(dve, ld_q1, j * 64)
                after(dve, ld_k1, j * 64)
                for m, (hi, lo) in enumerate(((q1h, q1l), (k1h, k1l))):
                    dve.wait_ge(ac_qk1h, j * 2 + m + 1)
                    v.scalar_tensor_tensor(out=lo[:], in0=PR[m][:], scalar=b1_sb[:, m:m + 1],
                                           in1=hi[:].bitcast(F32), op0=ALU.add,
                                           op1=ALU.subtract).then_inc(dv_qk1l, 1)

            dve.wait_ge(ld_first, 16 * 2)
            low_qk1(0)
            dve.wait_ge(set_w1, 1)
            v.tensor_tensor(w1l[:], w1_sb[:, 0:2], w1h[:].bitcast(F32), ALU.subtract).then_inc(set_w1, 1)

            def whole(w, n, bank, loaded):
                dve.wait_ge(loaded, 16)
                dve.wait_ge(set_bias, n + 1 if n < 3 * KT else n + 2)
                v.scalar_tensor_tensor(out=w, in0=bank[:, 0:w.shape[1]], scalar=LORA, in1=w, op0=ALU.mult,
                                       op1=ALU.add).then_inc(set_w, 1)

            for n in range(2 * KT):
                whole(wkv_sb[:, n // 2, n % 2, :], n, SN[n % 2], ld_wkv)
            for n in range(2 * KT, 3 * KT):
                whole(wq_sb[:, n - 2 * KT].rearrange("p r m -> p (r m)"), n, SN[n % 2], ld_wq)
            dve.wait_ge(set_bias, 3 * KT + 1)
            v.tensor_tensor(b1_sb[:, 3:4], SN[0][:, 0:1], b1_sb[:, 2:3], ALU.add).then_inc(set_w, 1)

            def whole_out(r):
                whole(wo_sb[:, r, :], 3 * KT + r, PR[r % 2], ld_wo)

            def split_out():
                flat = "p r n -> p (r n)"
                dve.wait_ge(set_w, LOWS + 1)
                v.tensor_copy(woh[:].rearrange(flat), wo_sb[:].rearrange(flat)).then_inc(set_wo, 1)
                dve.wait_ge(set_wo, 1)
                v.tensor_tensor(wol[:].rearrange(flat), wo_sb[:].rearrange(flat),
                                woh[:].bitcast(F32).rearrange(flat), ALU.subtract).then_inc(set_wo, 1)

            def alone():
                dve.wait_ge(ld_mask, 16)

            def split3(m, p, r, done, at):
                v.tensor_copy(p[0], m).then_inc(done, 1)
                dve.wait_ge(done, at + 1)
                v.tensor_tensor(r[0], m, p[0], ALU.subtract).then_inc(done, 1)
                dve.wait_ge(done, at + 2)
                v.tensor_copy(p[1], r[0]).then_inc(done, 1)
                dve.wait_ge(done, at + 3)
                v.tensor_tensor(r[1], r[0], p[1], ALU.subtract).then_inc(done, 1)
                dve.wait_ge(done, at + 4)
                v.tensor_copy(p[2], r[1]).then_inc(done, 1)

            def reciprocal0(j, half):
                dve.wait_ge(ac_w0, j + 1)
                cols = slice(half * P, (half + 1) * P)
                v.reciprocal(rec0[:, 1, cols], w0[:, 1, cols]).then_inc(dv_r0, 1)

            def normalise0(j, b, values):
                dve.wait_ge(dv_r0, j * 3 + (3 if b else 1))
                v.tensor_tensor(o0[:, :, b, :], values.rearrange("p (r q) -> p r q", r=REP),
                                rec0[:, b].rearrange("p (r q) -> p r q", r=REP), ALU.mult).then_inc(dv_n0, 1)

            def masked_y(j):
                dve.wait_ge(pe_o1, j + 1)
                dve.wait_ge(ld_mk, j * 32 + 32)
                v.scalar_tensor_tensor(out=y1[:], in0=PR[0][:], scalar=b1_sb[:, 3:4], in1=mk_sb[:], op0=ALU.add,
                                       op1=ALU.mult).then_inc(dv_y, 1)

            def sum_z(j):
                dve.wait_ge(po_y, j + 1)
                dve.wait_ge(pe_o0, j + 1)
                v.tensor_tensor(z[:], PR[1][:], y[:], ALU.add).then_inc(dv_z, 1)

            def statistics(j):
                dve.wait_ge(dv_z, j + 1)
                v.bn_stats(stats[:], z[:]).then_inc(dv_bn, 1)
                alone()
                dve.wait_ge(dv_bn, j + 1)
                v.bn_aggr(mv[:], stats[:]).then_inc(dv_st, 1)
                dve.wait_ge(dv_st, j * 2 + 1)
                v.tensor_scalar(vare[:], mv[:, 1:2], EPS, None, ALU.add).then_inc(dv_st, 1)

            def normalise(j):
                dve.wait_ge(po_rstd, j + 1)
                after(dve, st_out, j * 16)
                v.tensor_scalar(res[:], z[:], mv[:, 0:1], rstd[:, 0:1], ALU.subtract,
                                ALU.mult).then_inc(dv_out, 1)

            def step(i, first, more):
                for u in range(UNITS1):
                    if u < 2 and not first:
                        reciprocal0(i - 1, u)
                    dve.wait_ge(pe_sn, i * UNITS + u + 1)
                    v.tensor_reduce(m1[:, u // 4, (u % 4) * 8:(u % 4) * 8 + 8],
                                    SN[u % 2][:].rearrange("p (m t) -> p m t", t=CH), AX_X,
                                    ALU.max).then_inc(dv_mx, 1)
                    if u in (1, 2, 4, 5) and first:
                        whole_out({1: 0, 2: 1, 4: 2, 5: 3}[u])
                    if u == 1 and not first:
                        normalise0(i - 1, 1, w0[:, 0])
                    if u == 5 and not first:
                        masked_y(i - 1)
                    if u == 2 and more:
                        dve.wait_ge(ac_cnh, i + 1)
                        v.tensor_tensor(cnl[:], cn_sb[:], cnh[:].bitcast(F32), ALU.subtract).then_inc(dv_cnl, 1)
                    if u == 3:
                        dve.wait_ge(ac_v0, i * 4 + 4)
                        after(dve, ld_k0, i * 48)
                        v.tensor_tensor(k0l[:].rearrange("p b t -> p (b t)"), PV[0][:, 0:P],
                                        k0h[:].bitcast(F32).rearrange("p b t -> p (b t)"),
                                        ALU.subtract).then_inc(dv_k0l, 1)
                dve.wait_ge(dv_mx, i * UNITS + UNITS1)
                split3(m1[:], [m1p[:, :, k, :] for k in range(PARTS)], [m1r[:, k] for k in range(2)], dv_p1,
                       i * 5)
                for u in range(UNITS0):
                    dve.wait_ge(pe_sn, i * UNITS + UNITS1 + u + 1)
                    v.tensor_reduce(m0[:, u * NKV:(u + 1) * NKV],
                                    SN[u % 2][:].rearrange("p (m t) -> p m t", t=S), AX_X,
                                    ALU.max).then_inc(dv_mx, 1)
                    if u == 1:
                        dve.wait_ge(ac_q0h, i + 1)
                        after(dve, ld_q0, i * 48)
                        v.tensor_tensor(q0l[:].rearrange("p b r q -> p r b q"),
                                        PV[1][:].rearrange("p (r b q) -> p r b q", r=REP, b=2),
                                        q0h[:].bitcast(F32).rearrange("p b r q -> p r b q"),
                                        ALU.subtract).then_inc(dv_q0l, 1)
                    if u == 1 and not first:
                        sum_z(i - 1)
                    if u == 3 and more:
                        low_qk1(i + 1)
                dve.wait_ge(dv_mx, i * UNITS + UNITS)
                split3(m0[:], [m0p[:, k, :] for k in range(PARTS)], [m0r[:, k] for k in range(2)], dv_p0,
                       i * 5)
                if first:
                    split_out()
                else:
                    statistics(i - 1)

                for k in range(2):
                    even, odd = (PV[k][:].rearrange("p (n c o q) -> p o n c q", n=2, o=2, q=CH)[:, o] for o in range(2))
                    dve.wait_ge(ac_odd1, i * 2 + k + 1)
                    v.scalar_tensor_tensor(out=sum1[:, k].rearrange("p (n c q) -> p n c q", n=2, q=CH), in0=even,
                                           scalar=selr_sb[:, 1:2], in1=odd1[:, k], op0=ALU.mult,
                                           op1=ALU.add).then_inc(dv_s1, 1)
                    dve.wait_ge(dv_s1, i * 4 + 2 * k + 1)
                    v.reciprocal(rec1[:, k], sum1[:, k]).then_inc(dv_r1, 1)
                    alone()
                    dve.wait_ge(dv_r1, i * 2 + k + 1)
                    v.stream_shuffle(sum1[:, k], rec1[:, k], [(j + 16) % 32 for j in range(32)]).then_inc(dv_s1, 1)
                    dve.wait_ge(dv_s1, i * 4 + 2 * k + 2)
                    for o, part in enumerate((even, odd)):
                        v.scalar_tensor_tensor(out=o1n[:, k, o], in0=part, scalar=selr_sb[:, o:o + 1],
                                               in1=sum1[:, k].rearrange("p (n c q) -> p n c q", n=2, q=CH),
                                               op0=ALU.mult, op1=ALU.mult).then_inc(dv_n1, 1)
                    if k == 0 and not first:
                        normalise(i - 1)
                dve.wait_ge(pe_pv, i * UNITS + UNITS1 + 2)
                v.reciprocal(rec0[:, 0], SN[0][:, 256:512]).then_inc(dv_r0, 1)
                normalise0(i, 0, SN[0][:, 0:256])

            step(0, True, True)
            with dve.Fori(1, PAIRS - 1) as i:
                step(i, False, True)
            step(PAIRS - 1, False, False)
            reciprocal0(PAIRS - 1, 0)
            reciprocal0(PAIRS - 1, 1)
            normalise0(PAIRS - 1, 1, w0[:, 0])
            masked_y(PAIRS - 1)
            sum_z(PAIRS - 1)
            statistics(PAIRS - 1)
            normalise(PAIRS - 1)


def lay_out(inp):
    import numpy as np

    def bf16(a):
        return (np.asarray(a, np.float32).view(np.uint32) >> 16).astype(np.uint16)

    x, c = np.asarray(inp["x"]), np.asarray(inp["ctx_4096"])

    def turned(a):
        return np.ascontiguousarray(a.reshape(PAIRS, P, KT, P).transpose(0, 3, 2, 1)).reshape(PAIRS * P, KT, P)

    def by_r(a, axis):
        s = a.shape
        a = a.reshape(s[:axis] + (NKV, REP, HD) + s[axis + 1:])
        return np.swapaxes(a, axis, axis + 1).reshape(s)

    def by_half(a):
        return a.reshape(-1, 4, 2, HD).transpose(0, 2, 1, 3).reshape(-1, P)

    g = {k[9:]: np.asarray(v) for k, v in inp.items() if k.startswith("L0_xattn_") or k.startswith("L1_xattn_")}
    out = {
        "xT": turned(x), "xn": x.reshape(N * S, H), "cT": turned(c), "cn": c.reshape(N * S, H),
        "mask": np.asarray(inp["mask_Bx1x4096_ff1"]).reshape(N, H),
        "wq": by_r(g["Wq"], 1).reshape(KT, P, REP, P).transpose(1, 0, 2, 3),
        "wkv": np.stack([g["Wk"], by_half(g["Wv"])], 1).reshape(KT, P, 2, P).transpose(1, 0, 2, 3),
        "wo": by_r(g["Wo"], 0).reshape(REP, P, H).transpose(1, 0, 2),
        "low": np.concatenate([np.stack([g["Ak"].T, g["Av"].T], 1).reshape(R, 2, KT, P).transpose(0, 2, 1, 3)
                               .reshape(R, -1), g["Aq"].T, by_r(g["Ao"], 0).T,
                               g["Bk"], by_half(g["Bv"]), by_r(g["Bq"], 1), g["Bo"]], 1),
    }
    win, bin_, wout, bout = g["W_in"], g["b_in"], g["W_out"], g["b_out"]
    C = 64
    w1 = []
    for k in range(3):
        w = win[k * C:(k + 1) * C]
        both = np.zeros((2, C, 2, C), np.float32)
        for n in range(2):
            both[n, :, n, :] = w.T
        if k == 2:
            both = both.reshape(2, C, 2, 2, 4 * HD1).transpose(0, 1, 3, 2, 4)
        w1.append(both.reshape(P, P))
    out["w1"] = np.stack(w1, 1)
    out["b1v"] = bin_[2 * C:].reshape(C, 1)
    out["w1bias"] = np.concatenate([wout.T, wout.T], 1)
    w1o = np.zeros((2, 4, QD, C), np.float32)
    for k in range(2):
        w1o[k, :, k * 16:(k + 1) * 16] = wout.T.reshape(2, 4, HD1, C).transpose(1, 0, 2, 3).reshape(4, 16, C)
    rows = np.arange(P)
    biases = [np.tile(b, 2).reshape(P, 1) for b in (bin_[0:C], bin_[C:2 * C], bout, np.zeros(C, np.float32))]
    out["consts"] = np.concatenate(biases + [
        (rows[:, None] // HD == np.arange(NKV)).astype(np.float32),
        (rows[:, None] // HD1 % 4 == np.arange(4)).astype(np.float32),
        (rows[:, None] // 32 == np.arange(4)).astype(np.float32),
        (rows[:, None] // 32 % 2 == np.arange(2)).astype(np.float32),
        (rows[:, None] // HD % 2 == np.arange(2)).astype(np.float32),
        np.repeat((rows[:, None] // S == np.arange(2)).astype(np.float32), HD, 1),
        w1o[0].reshape(P, C), w1o[1].reshape(P, C)], 1)

    f0 = np.zeros((PARTS, 2, 2, NKV, 2, 2, 4, 2, S), np.float32)
    for b in range(2):
        for rp in range(2):
            for h in range(NKV):
                f0[:, b, rp, h, b, rp, h // 2, h % 2, :] = -1
    folds = np.zeros((P, 18, P), np.float32)
    folds[0:MROWS, 0:16] = f0.reshape(MROWS, 16, P)
    f1 = np.zeros((PARTS, 4, 2, 2, 2, 2, 4, 2, 2, CH), np.float32)
    for c4 in range(4):
        for hp in range(2):
            for n in range(2):
                for half in range(2):
                    f1[:, c4, hp, n, half, hp, c4, n, half, :] = -1
    fold1 = np.zeros((P, 2, 4 * 2 * 2 * CH), np.float32)
    fold1[0:MROWS] = f1.reshape(MROWS, 2, 4 * 2 * 2 * CH)
    out["fold1"] = bf16(fold1)
    neg = np.full(P, -1e9 / SCALE1, np.float32)
    negc = np.zeros((P, P), np.float32)
    for k in range(PARTS):
        negc[MROWS + k] = (neg.view(np.uint32) & 0xFFFF0000).view(np.float32)
        neg = neg - negc[MROWS + k]
    folds[:, 16] = negc
    folds[:, 17] = np.eye(P)
    out["folds"] = bf16(folds)
    o1 = np.zeros((2, CH, NC, 2, 4, 2, 2, HD1), np.float32)
    for half in range(2):
        o1[half, :, 0::2, :, :, 1, half, :] = 1
        o1[half, :, 1::2, :, :, 0, half, :] = 1
    out["ones1"] = o1.reshape(P, NC, 2, 4, QD)
    return {k: np.ascontiguousarray(v) for k, v in out.items()}


def kernel(**inputs):
    import concourse.bacc as _bacc
    from concourse.bass_utils import run_bass_kernel_spmd as _run

    nc = _bacc.Bacc("TRN2", target_bir_lowering=False, num_devices=1)
    arrays = lay_out(inputs)
    args = {k: nc.dram_tensor(f"in_{k}", a.shape, mybir.dt.from_np(a.dtype), kind="ExternalInput").ap()
            for k, a in arrays.items()}
    out = nc.dram_tensor("out", (N * S, H), F32, kind="ExternalOutput").ap()
    build(nc, out=out, **args)
    r = _run(nc, [{f"in_{k}": a for k, a in arrays.items()}], core_ids=[0])
    return r.results[0]["out"].reshape(N, S, H)
```
